# Optimizing a Trainium2 kernel written in Bass

```python
import numpy as np
import jax
import jax.numpy as jnp

def _softmax(x, axis=-1):
    return jax.nn.softmax(x, axis=axis)

def _gelu(x):
    return jax.nn.gelu(x, approximate=True)

def _silu(x):
    return jax.nn.silu(x)

def _sigmoid(x):
    return jax.nn.sigmoid(x)

def _layernorm(x, axis=-1, eps=1e-05):
    m = jnp.mean(x, axis=axis, keepdims=True)
    v = jnp.var(x, axis=axis, keepdims=True)
    return (x - m) / jnp.sqrt(v + eps)

def _scatter_add(tgt, idx, src, axis=0):
    return tgt.at[idx].add(src)

def _segment_sum(src, seg, n):
    return jax.ops.segment_sum(src, seg, n)
kernel_name = 'mk_gnn_resnorm_d4_gnn_r8_5d72dd'

def setup_inputs(seed: int=0):
    np.random.seed(seed)
    _w = jnp.asarray

    def _rec_inputs():
        import jax
        import jax.numpy as jnp
        _gk = jax.random.key(seed)
        x = -0.000202 + 1 * jax.random.normal(jax.random.fold_in(_gk, 1), (6250, 128), jnp.float32)
        _s = jax.random.randint(jax.random.fold_in(_gk, 2), (50000,), 0, 6250, jnp.int32)
        _d = jax.random.randint(jax.random.fold_in(_gk, 3), (50000,), 0, 6250, jnp.int32)
        _loop = jnp.arange(6250, dtype=jnp.int32)
        src = jnp.concatenate([_s, _d, _loop])
        dst = jnp.concatenate([_d, _s, _loop])
        _o = jnp.argsort(dst, stable=True)
        src = src[_o]
        dst = dst[_o]
        edge_attr_32 = 0.000189758 + 1.00013 * jax.random.normal(jax.random.fold_in(_gk, 12), (106250, 32), jnp.float32)
        edge_type_8 = jax.random.randint(jax.random.fold_in(_gk, 14), (106250,), 0, 8, jnp.int32)
        return (x, src, dst, edge_attr_32, edge_type_8)
    x, src, dst, edge_attr_32, edge_type_8 = _rec_inputs()

    def _L0_gnn_setup():
        import jax, jax.numpy as jnp
        import numpy as np
        N = 6250
        E = 75000
        IN = 128
        H = 4
        C = 32
        B = 3
        NEG_SLOPE = 0.2
        key = jax.random.key(seed)
        ks = jax.random.split(key, 6)
        x = jax.random.normal(ks[0], (N, IN), dtype=jnp.float32)
        edge_index = jax.random.randint(ks[1], (2, E), 0, N)
        coeffs_t = jnp.array([0.25, 0.5, 0.25], dtype=jnp.float32)
        glorot_w = float(np.sqrt(2.0) * np.sqrt(6.0 / (H * C + IN)))
        glorot_a = float(np.sqrt(2.0) * np.sqrt(6.0 / (1 + C)))
        lin_weight = jax.random.uniform(ks[2], (B, H * C, IN), jnp.float32, -glorot_w, glorot_w)
        lin_bias = jnp.zeros((B, H * C), dtype=jnp.float32)
        att_src = jax.random.uniform(ks[3], (B, 1, H, C), jnp.float32, -glorot_a, glorot_a)
        att_dst = jax.random.uniform(ks[4], (B, 1, H, C), jnp.float32, -glorot_a, glorot_a)
        return {'x': x, 'edge_index': edge_index, 'coeffs_t': coeffs_t, 'lin_weight': lin_weight, 'lin_bias': lin_bias, 'att_src': att_src, 'att_dst': att_dst}
    _L0_gnn_all = _L0_gnn_setup()
    _L0_gnn_in = {k: v for k, v in _L0_gnn_all.items() if k in ('coeffs_t', 'lin_weight', 'lin_bias', 'att_src', 'att_dst')}
    del _L0_gnn_all

    def _L1_gnn_setup():
        import jax, jax.numpy as jnp
        import numpy as np
        N_NODES = 12500
        N_EDGES = 200000
        IN_DIM = 128
        OUT_DIM = 128
        EDGE_DIM = 32
        EPS = 1e-05

        def _layernorm(h, gamma, beta):
            mu = jnp.mean(h, axis=-1, keepdims=True)
            var = jnp.var(h, axis=-1, keepdims=True)
            return (h - mu) * jax.lax.rsqrt(var + EPS) * gamma + beta
        key = jax.random.key(seed)
        ks = jax.random.split(key, 10)
        hid = OUT_DIM * 2
        x = jax.random.normal(ks[0], (N_NODES, IN_DIM), dtype=jnp.float32)
        edge_index = jax.random.randint(ks[1], (2, N_EDGES), 0, N_NODES, dtype=jnp.int64)
        edge_attr = jax.random.normal(ks[2], (N_EDGES, EDGE_DIM), dtype=jnp.float32)
        W1 = jax.random.normal(ks[3], (IN_DIM + EDGE_DIM, hid), dtype=jnp.float32) / np.sqrt(IN_DIM + EDGE_DIM)
        b1 = jnp.zeros((hid,), jnp.float32)
        g1 = jnp.ones((hid,), jnp.float32)
        be1 = jnp.zeros((hid,), jnp.float32)
        W2 = jax.random.normal(ks[4], (hid, OUT_DIM), dtype=jnp.float32) / np.sqrt(hid)
        b2 = jnp.zeros((OUT_DIM,), jnp.float32)
        Wu = jax.random.normal(ks[5], (IN_DIM + OUT_DIM, OUT_DIM), dtype=jnp.float32) / np.sqrt(IN_DIM + OUT_DIM)
        bu = jnp.zeros((OUT_DIM,), jnp.float32)
        gu = jnp.ones((OUT_DIM,), jnp.float32)
        beu = jnp.zeros((OUT_DIM,), jnp.float32)
        return {'x': x, 'edge_index': edge_index, 'edge_attr': edge_attr, 'W1': W1, 'b1': b1, 'g1': g1, 'be1': be1, 'W2': W2, 'b2': b2, 'Wu': Wu, 'bu': bu, 'gu': gu, 'beu': beu}
    _L1_gnn_all = _L1_gnn_setup()
    _L1_gnn_in = {k: v for k, v in _L1_gnn_all.items() if k in ('W1', 'b1', 'g1', 'be1', 'W2', 'b2', 'Wu', 'bu', 'gu', 'beu')}
    del _L1_gnn_all

    def _L2_gnn_setup():
        import jax, jax.numpy as jnp
        import numpy as np
        N_NODES = 6250
        N_EDGES = 75000
        IN_FEAT = 128
        OUT_FEAT = 128
        NUM_RELS = 8
        key = jax.random.key(seed)
        ks = jax.random.split(key, 9)
        return {'h': jax.random.normal(ks[0], (N_NODES, IN_FEAT), dtype=jnp.float32), 'W': jax.random.normal(ks[1], (NUM_RELS, IN_FEAT, OUT_FEAT), dtype=jnp.float32) * 0.05, 'bias_term': jax.random.normal(ks[2], (NUM_RELS, OUT_FEAT), dtype=jnp.float32) * 0.05, 'gate_weight': jax.random.normal(ks[3], (NUM_RELS, OUT_FEAT, 1), dtype=jnp.float32) * 0.05, 'gate_bias': jax.random.normal(ks[4], (NUM_RELS, 1), dtype=jnp.float32) * 0.05, 'loop_weight': jax.random.normal(ks[5], (IN_FEAT, OUT_FEAT), dtype=jnp.float32) * 0.05, 'src': jax.random.randint(ks[6], (N_EDGES,), 0, N_NODES, dtype=jnp.int32), 'dst': jax.random.randint(ks[7], (N_EDGES,), 0, N_NODES, dtype=jnp.int32), 'rel': jax.random.randint(ks[8], (N_EDGES,), 0, NUM_RELS, dtype=jnp.int32)}
    _L2_gnn_all = _L2_gnn_setup()
    _L2_gnn_in = {k: v for k, v in _L2_gnn_all.items() if k in ('W', 'bias_term', 'gate_weight', 'gate_bias', 'loop_weight')}
    del _L2_gnn_all

    def _L3_gnn_setup():
        import jax, jax.numpy as jnp
        import numpy as np
        N_NODES = 12500
        N_EDGES = 200000
        IN_DIM = 128
        OUT_DIM = 32
        HEADS = 4
        NEG_SLOPE = 0.2
        EPS = 1e-16

        def _gat_layer(x, edge_index, W, att_src, att_dst, bias, gamma, beta):
            N = x.shape[0]
            H, C = (att_src.shape[1], att_src.shape[2])
            loop = jnp.arange(N, dtype=edge_index.dtype)
            src = jnp.concatenate([edge_index[0], loop])
            dst = jnp.concatenate([edge_index[1], loop])
            h = (x @ W).reshape(N, H, C)
            a_src = jnp.sum(h * att_src, axis=-1)
            a_dst = jnp.sum(h * att_dst, axis=-1)
            logits = a_src[src] + a_dst[dst]
            logits = jnp.where(logits > 0, logits, NEG_SLOPE * logits)
            seg_max = jax.ops.segment_max(logits, dst, num_segments=N)
            e = jnp.exp(logits - seg_max[dst])
            denom = jax.ops.segment_sum(e, dst, num_segments=N)
            alpha = e / (denom[dst] + EPS)
            msgs = h[src] * alpha[:, :, None]
            out = jax.ops.segment_sum(msgs, dst, num_segments=N)
            out = out.reshape(N, H * C) + bias
            mu = jnp.mean(out, axis=-1, keepdims=True)
            var = jnp.var(out, axis=-1, keepdims=True)
            out = (out - mu) * jax.lax.rsqrt(var + 1e-05) * gamma + beta
            return jax.nn.relu(out)
        key = jax.random.key(seed)
        ks = jax.random.split(key, 8)
        x = jax.random.normal(ks[0], (N_NODES, IN_DIM), dtype=jnp.float32)
        edge_index = jax.random.randint(ks[1], (2, N_EDGES), 0, N_NODES, dtype=jnp.int64)
        glorot = 1.0 / np.sqrt(IN_DIM)
        W = jax.random.uniform(ks[2], (IN_DIM, HEADS * OUT_DIM), dtype=jnp.float32, minval=-glorot, maxval=glorot)
        ga = 1.0 / np.sqrt(OUT_DIM)
        att_src = jax.random.uniform(ks[3], (1, HEADS, OUT_DIM), dtype=jnp.float32, minval=-ga, maxval=ga)
        att_dst = jax.random.uniform(ks[4], (1, HEADS, OUT_DIM), dtype=jnp.float32, minval=-ga, maxval=ga)
        bias = jnp.zeros((HEADS * OUT_DIM,), dtype=jnp.float32)
        gamma = jnp.ones((HEADS * OUT_DIM,), dtype=jnp.float32)
        beta = jnp.zeros((HEADS * OUT_DIM,), dtype=jnp.float32)
        return {'x': x, 'edge_index': edge_index, 'W': W, 'att_src': att_src, 'att_dst': att_dst, 'bias': bias, 'gamma': gamma, 'beta': beta}
    _L3_gnn_all = _L3_gnn_setup()
    _L3_gnn_in = {k: v for k, v in _L3_gnn_all.items() if k in ('W', 'att_src', 'att_dst', 'bias', 'gamma', 'beta')}
    del _L3_gnn_all
    return {'x': x, 'src': src, 'dst': dst, 'edge_attr_32': edge_attr_32, 'edge_type_8': edge_type_8, 'L0_gnn_coeffs_t': _L0_gnn_in['coeffs_t'], 'L0_gnn_lin_weight': _L0_gnn_in['lin_weight'], 'L0_gnn_lin_bias': _L0_gnn_in['lin_bias'], 'L0_gnn_att_src': _L0_gnn_in['att_src'], 'L0_gnn_att_dst': _L0_gnn_in['att_dst'], 'L1_gnn_W1': _L1_gnn_in['W1'], 'L1_gnn_b1': _L1_gnn_in['b1'], 'L1_gnn_g1': _L1_gnn_in['g1'], 'L1_gnn_be1': _L1_gnn_in['be1'], 'L1_gnn_W2': _L1_gnn_in['W2'], 'L1_gnn_b2': _L1_gnn_in['b2'], 'L1_gnn_Wu': _L1_gnn_in['Wu'], 'L1_gnn_bu': _L1_gnn_in['bu'], 'L1_gnn_gu': _L1_gnn_in['gu'], 'L1_gnn_beu': _L1_gnn_in['beu'], 'L2_gnn_W': _L2_gnn_in['W'], 'L2_gnn_bias_term': _L2_gnn_in['bias_term'], 'L2_gnn_gate_weight': _L2_gnn_in['gate_weight'], 'L2_gnn_gate_bias': _L2_gnn_in['gate_bias'], 'L2_gnn_loop_weight': _L2_gnn_in['loop_weight'], 'L3_gnn_W': _L3_gnn_in['W'], 'L3_gnn_att_src': _L3_gnn_in['att_src'], 'L3_gnn_att_dst': _L3_gnn_in['att_dst'], 'L3_gnn_bias': _L3_gnn_in['bias'], 'L3_gnn_gamma': _L3_gnn_in['gamma'], 'L3_gnn_beta': _L3_gnn_in['beta']}

def reference(x, src, dst, edge_attr_32, edge_type_8, L0_gnn_coeffs_t, L0_gnn_lin_weight, L0_gnn_lin_bias, L0_gnn_att_src, L0_gnn_att_dst, L1_gnn_W1, L1_gnn_b1, L1_gnn_g1, L1_gnn_be1, L1_gnn_W2, L1_gnn_b2, L1_gnn_Wu, L1_gnn_bu, L1_gnn_gu, L1_gnn_beu, L2_gnn_W, L2_gnn_bias_term, L2_gnn_gate_weight, L2_gnn_gate_bias, L2_gnn_loop_weight, L3_gnn_W, L3_gnn_att_src, L3_gnn_att_dst, L3_gnn_bias, L3_gnn_gamma, L3_gnn_beta):
    import jax
    import jax.numpy as jnp

    def _L0_gnn_ref(x, edge_index, coeffs_t, lin_weight, lin_bias, att_src, att_dst):
        import jax, jax.numpy as jnp
        import numpy as np
        N = 6250
        E = 75000
        IN = 128
        H = 4
        C = 32
        B = 3
        NEG_SLOPE = 0.2
        W = jnp.einsum('b,boi->oi', coeffs_t, lin_weight)
        bias = jnp.einsum('b,bo->o', coeffs_t, lin_bias)
        a_src = jnp.einsum('b,bqhc->qhc', coeffs_t, att_src)
        a_dst = jnp.einsum('b,bqhc->qhc', coeffs_t, att_dst)
        n = x.shape[0]
        xt = (x @ W.T + bias).reshape(n, H, C)
        alpha_src = jnp.sum(xt * a_src, axis=-1)
        alpha_dst = jnp.sum(xt * a_dst, axis=-1)
        row, col = (edge_index[0], edge_index[1])
        alpha = alpha_src[row] + alpha_dst[col]
        alpha = jax.nn.leaky_relu(alpha, NEG_SLOPE)
        amax = jax.ops.segment_max(alpha, col, num_segments=n)
        ex = jnp.exp(alpha - amax[col])
        denom = jax.ops.segment_sum(ex, col, num_segments=n)
        alpha = ex / (denom[col] + 1e-16)
        msg = xt[row] * alpha[..., None]
        out = jax.ops.segment_sum(msg, col, num_segments=n)
        return out.reshape(n, H * C)

    def _L1_gnn_ref(x, edge_index, edge_attr, W1, b1, g1, be1, W2, b2, Wu, bu, gu, beu):
        import jax, jax.numpy as jnp
        import numpy as np
        N_NODES = 12500
        N_EDGES = 200000
        IN_DIM = 128
        OUT_DIM = 128
        EDGE_DIM = 32
        EPS = 1e-05

        def _layernorm(h, gamma, beta):
            mu = jnp.mean(h, axis=-1, keepdims=True)
            var = jnp.var(h, axis=-1, keepdims=True)
            return (h - mu) * jax.lax.rsqrt(var + EPS) * gamma + beta
        row, col = (edge_index[0], edge_index[1])
        msg_in = jnp.concatenate([x[row], edge_attr], axis=-1)
        h = msg_in @ W1 + b1
        h = jax.nn.gelu(_layernorm(h, g1, be1), approximate=False)
        msg = h @ W2 + b2
        agg = jax.ops.segment_sum(msg, col, num_segments=x.shape[0])
        u = jnp.concatenate([x, agg], axis=-1) @ Wu + bu
        u = jax.nn.gelu(_layernorm(u, gu, beu), approximate=False)
        return u + x

    def _L2_gnn_ref(h, W, bias_term, gate_weight, gate_bias, loop_weight, src, dst, rel):
        import jax, jax.numpy as jnp
        import numpy as np
        N_NODES = 6250
        N_EDGES = 75000
        IN_FEAT = 128
        OUT_FEAT = 128
        NUM_RELS = 8
        n_nodes = h.shape[0]
        loop_message = h @ loop_weight
        xw = jnp.einsum('ni,rio->rno', h, W)
        msg = xw[rel, src] + bias_term[rel]
        gw = gate_weight[..., 0]
        gate = jax.nn.sigmoid(jnp.sum(msg * gw[rel], axis=-1) + gate_bias[rel, 0])
        agg = jax.ops.segment_sum(msg * gate[:, None], dst, num_segments=n_nodes)
        node_repr = agg + loop_message
        return jax.nn.relu(node_repr)

    def _L3_gnn_ref(x, edge_index, W, att_src, att_dst, bias, gamma, beta):
        import jax, jax.numpy as jnp
        import numpy as np
        N_NODES = 12500
        N_EDGES = 200000
        IN_DIM = 128
        OUT_DIM = 32
        HEADS = 4
        NEG_SLOPE = 0.2
        EPS = 1e-16

        def _gat_layer(x, edge_index, W, att_src, att_dst, bias, gamma, beta):
            N = x.shape[0]
            H, C = (att_src.shape[1], att_src.shape[2])
            loop = jnp.arange(N, dtype=edge_index.dtype)
            src = jnp.concatenate([edge_index[0], loop])
            dst = jnp.concatenate([edge_index[1], loop])
            h = (x @ W).reshape(N, H, C)
            a_src = jnp.sum(h * att_src, axis=-1)
            a_dst = jnp.sum(h * att_dst, axis=-1)
            logits = a_src[src] + a_dst[dst]
            logits = jnp.where(logits > 0, logits, NEG_SLOPE * logits)
            seg_max = jax.ops.segment_max(logits, dst, num_segments=N)
            e = jnp.exp(logits - seg_max[dst])
            denom = jax.ops.segment_sum(e, dst, num_segments=N)
            alpha = e / (denom[dst] + EPS)
            msgs = h[src] * alpha[:, :, None]
            out = jax.ops.segment_sum(msgs, dst, num_segments=N)
            out = out.reshape(N, H * C) + bias
            mu = jnp.mean(out, axis=-1, keepdims=True)
            var = jnp.var(out, axis=-1, keepdims=True)
            out = (out - mu) * jax.lax.rsqrt(var + 1e-05) * gamma + beta
            return jax.nn.relu(out)
        return _gat_layer(x, edge_index, W, att_src, att_dst, bias, gamma, beta)
    edge_index = jnp.stack([src, dst])
    x = _layernorm(x + _L0_gnn_ref(x, edge_index, L0_gnn_coeffs_t, L0_gnn_lin_weight, L0_gnn_lin_bias, L0_gnn_att_src, L0_gnn_att_dst), axis=-1)
    x = _layernorm(x + _L1_gnn_ref(x, edge_index, edge_attr_32, L1_gnn_W1, L1_gnn_b1, L1_gnn_g1, L1_gnn_be1, L1_gnn_W2, L1_gnn_b2, L1_gnn_Wu, L1_gnn_bu, L1_gnn_gu, L1_gnn_beu), axis=-1)
    x = _layernorm(x + _L2_gnn_ref(x, L2_gnn_W, L2_gnn_bias_term, L2_gnn_gate_weight, L2_gnn_gate_bias, L2_gnn_loop_weight, src, dst, edge_type_8), axis=-1)
    x = _layernorm(x + _L3_gnn_ref(x, edge_index, L3_gnn_W, L3_gnn_att_src, L3_gnn_att_dst, L3_gnn_bias, L3_gnn_gamma, L3_gnn_beta), axis=-1)
    return x

_drawn_inputs = setup_inputs


def setup_inputs(seed=0):
    import zlib

    import numpy as np

    out = dict(_drawn_inputs(seed))
    spreads = {'L0_gnn_lin_bias': (0.0, 0.1),
     'L1_gnn_b1': (0.0, 0.1),
     'L1_gnn_g1': (1.0, 0.2),
     'L1_gnn_be1': (0.0, 0.1),
     'L1_gnn_b2': (0.0, 0.1),
     'L1_gnn_bu': (0.0, 0.525),
     'L1_gnn_gu': (1.0, 0.2),
     'L1_gnn_beu': (0.0, 0.1),
     'L3_gnn_bias': (0.0, 0.1),
     'L3_gnn_gamma': (1.0, 0.2),
     'L3_gnn_beta': (0.0, 0.1)}
    factors = {'L2_gnn_gate_bias': 2.728}
    for name, (base, spread) in spreads.items():
        noise = np.random.default_rng([zlib.crc32(name.encode()), seed]).standard_normal(out[name].shape)
        drawn = base * np.exp(spread * noise) if base else spread * noise
        out[name] = jnp.asarray(drawn.astype(out[name].dtype))
    for name, factor in factors.items():
        out[name] = (out[name] * factor).astype(out[name].dtype)
    return out
```

```python
import concourse.bass as bass
from concourse import mybir
import numpy as np
from collections import namedtuple
from contextlib import ExitStack, contextmanager


F32 = mybir.dt.float32
I32 = mybir.dt.int32
ALU = mybir.AluOpType
ACT = mybir.ActivationFunctionType
AX = mybir.AxisListType
MAX_OVER_PARTITIONS = bass.bass_isa.ReduceOp.max

P = 128
F = 128
H = 4
C = F // H
HID = 2 * F
ED = 32
R = 8
T = 8
STACK = P // 32
GE = T * P
RING = 4
TAB = 136
ONE, AS = F, F + 1
SUMS = AS + H
EPS = 1e-5
SOFTMAX_EPS = 1e-16
SLOPE = 0.2
SPREAD = 40.0
RSQRT_SEED = 0x5F3759DF
BIG = 3.0e38

Shapes = namedtuple("Shapes", "N E NT NP NW NG NB NBATCH BN")
Step = namedtuple("Step", "n slot visit group col base")


def shapes_of(n, e):
    nb = 7
    nt = -(-n // (P * nb)) * nb
    if n == nt * P:
        nt += nb
    ng = -(-e // (GE * RING)) * RING
    return Shapes(n, e, nt, nt * P, nt * P + P, ng, nb, nt // nb, nb * P)


def wait(eng, sem, value):
    if isinstance(value, int) and value <= 0:
        return
    eng.wait_ge(sem, value)


def drive(eng, sh, stages, fast):
    if not fast:
        with eng.Fori(0, sh.NG) as g:
            with eng.Fori(0, sh.NT) as k:
                for stage, lags in stages:
                    stage(*[Step(g * sh.NT + k, 0, g * sh.NT + k, g, k, k * P)] * len(lags))
        return

    def at(n, k, visit):
        for stage, lags in stages:
            steps = []
            for lag in lags:
                inside = not isinstance(n, int) or 0 <= n - lag < sh.NG
                steps.append(Step(n - lag, (k - lag) % RING, visit + (k - lag) // RING, n - lag, n - lag, None) if inside else None)
            if any(st is not None for st in steps):
                stage(*steps)

    most = max(max(lags) for _, lags in stages)
    for n in range(RING):
        at(n, n, 0)
    if sh.NG > RING:
        with eng.Fori(1, sh.NG // RING) as i:
            for k in range(RING):
                at(i * RING + k, k, i)
    for n in range(sh.NG, sh.NG + most):
        at(n, n % RING, n // RING)


class Net:

    def __init__(self, nc, ctx, sh, ins, out):
        self.nc, self.ctx, self.sh, self.ins, self.out = nc, ctx, sh, ins, out
        self.phases = 0

        def sb(name, shape, dt=F32):
            return ctx.enter_context(nc.sbuf_tensor(name, shape, dt))

        self.x = sb("x_nodes", [P, sh.NT, F])
        self.acc = sb("acc_t", [P, 2, sh.NW])
        self.h_self = self.acc[:, 1, 0:sh.NT * P].rearrange("p (t f) -> p t f", f=F)
        self.den = sb("den_t", [1 + H, sh.NW])
        self.adc = sb("adc", [P, sh.NT, 2 * H])
        self.a_self = sb("a_self", [P, sh.NT, H])
        self.ident = sb("ident", [P, P])
        self.iota_row = sb("iota_row", [P, P])
        self.iota_col = sb("iota_col", [P, 1])
        self.ones_row = sb("ones_row", [1, P])
        self.gat_w = [sb(f"gat_w{l}", [P, TAB + 1]) for l in range(2)]
        self.gat_row = sb("gat_row", [P, TAB + 1])
        self.fast_base = sb("fast_base", [P, sh.NG])
        self.slow_base = sb("slow_base", [P, sh.NT])
        self.base_i = sb("base_i", [1, sh.NG], I32)
        self.fits = sb("fits", [1, 1], I32)
        self.narrow = sb("narrow", [1, 1], I32)

        def dram(name, shape, dt=F32):
            return nc.dram_tensor(name, shape, dt, kind="Internal").ap()

        self.gat_table = dram("gat_table", (sh.NP, TAB))
        self.adc_table = dram("adc_table", (sh.NW, 2 * H))
        self.mlp_table = dram("mlp_table", (sh.NP, HID))
        self.rel_table = dram("rel_table", (sh.NP * R, F))
        self.rel_index = dram("rel_index", (sh.NG, P, T), I32)


@contextmanager
def phase(net, names, rings=()):
    nc = net.nc
    net.phases += 1
    tag = f"_{net.phases}"
    sems = {n: nc.alloc_semaphore(n + tag) for n in names}
    for n in rings:
        sems[n] = [nc.alloc_semaphore(f"{n}{i}{tag}") for i in range(RING)]
    handles = []
    for s in sems.values():
        handles += s if isinstance(s, list) else [s]
    with ExitStack() as ctx:
        def sb(name, shape, dt=F32):
            return ctx.enter_context(nc.sbuf_tensor(name + tag, shape, dt))

        def ps(name, shape):
            return ctx.enter_context(nc.psum_tensor(name + tag, shape, F32))

        scope = namedtuple("Scope", ["sb", "ps", "block"] + list(sems))
        with nc.Block() as block:
            yield scope(sb, ps, block, **sems)
    nc.clear_and_free_semaphores(handles)
    nc.all_engine_barrier()


def spread(ap, shape):
    return ap.broadcast_to(shape)


def tiled(ap, n, width):
    return ap.unsqueeze(2).broadcast_to([P, n, width])


def over_tiles(ap, n, width):
    return ap.unsqueeze(1).broadcast_to([P, n, width])


RSQRT_STEPS = 11


def rsqrt_step(nc, j, y, work, v, half):
    dve = nc.vector
    if j == 0:
        return dve.tensor_scalar(half.bitcast(I32), v.bitcast(I32), 1, None, ALU.logical_shift_right)
    if j == 1:
        return dve.tensor_scalar(y.bitcast(I32), half.bitcast(I32), -1.0, float(RSQRT_SEED), ALU.mult, ALU.add)
    if j % 3 == 2:
        return dve.tensor_tensor(work, y, y, ALU.mult)
    if j % 3 == 0:
        return dve.scalar_tensor_tensor(half, work, -0.5, v, ALU.mult, ALU.mult)
    return dve.scalar_tensor_tensor(y, half, 1.5, y, ALU.add, ALU.mult)


def layer_norm(nc, out, v, square, stats, n):
    dve = nc.vector
    mean, var, y, work, half = (stats[:, k, 0:n] for k in range(5))
    dve.tensor_reduce(mean, v, AX.X, ALU.add)
    dve.drain()
    dve.tensor_scalar(mean, mean, 1.0 / F, None, ALU.mult)
    dve.drain()
    dve.tensor_tensor(v, v, tiled(mean, n, F), ALU.subtract)
    dve.drain()
    dve.tensor_tensor(square, v, v, ALU.mult)
    dve.drain()
    dve.tensor_reduce(var, square, AX.X, ALU.add)
    dve.drain()
    dve.tensor_scalar(var, var, 1.0 / F, EPS, ALU.mult, ALU.add)
    dve.drain()
    for j in range(RSQRT_STEPS):
        rsqrt_step(nc, j, y, work, var, half)
        dve.drain()
    return dve.tensor_tensor(out, v, tiled(y, n, F), ALU.mult)



def prepare(net):
    nc, sh, a = net.nc, net.sh, net.ins
    names = ["loaded", "combined", "turned", "turned_copied", "folded", "folded_copied",
             "checked", "check_copied", "check_turned", "index_in", "index_done", "index_out",
             "flag_max", "flag_row"]
    with phase(net, names) as s:
        lw = s.sb("lin_w", [P, 3, F])
        mix = s.sb("mix", [P, 3])
        wo = s.sb("w_out_in", [P, 2, F])
        wi = s.sb("w_in_out", [P, F])
        att = s.sb("att_cols", [P, 2, 3])
        att3 = s.sb("att3_cols", [P, 2])
        acol = s.sb("acol", [P, 2, 2])
        heads = s.sb("heads", [P, H])
        fold = s.sb("fold", [P, 2, 2 * H])
        bcols = s.sb("bias_cols", [P, 3])
        bcol = s.sb("bias_col", [P, 1])
        brow3 = s.sb("bias_rows", [1, 3, F])
        row = s.sb("row", [1, TAB + 1])
        tmp = s.sb("tmp", [P, 3])
        dst_i = s.sb("dst_i", [P, sh.NG, T], I32)
        src_i = s.sb("src_i", [P, sh.NG, T], I32)
        typ_i = s.sb("typ_i", [P, sh.NG, T], I32)
        rel = s.sb("rel", [P, sh.NG, T])
        base_row = s.sb("base_row", [1, sh.NG])
        worst = s.sb("worst", [P, 2])
        worst_all = s.sb("worst_all", [P, 1])
        slow_i = s.sb("slow_i", [P, sh.NT], I32)
        pt = s.ps("pt", [P, 2, P])
        pf = s.ps("pf", [P, 512])
        pr = s.ps("pr", [P, 512])
        pb = s.ps("pb", [P, 512])
        LOADS = 20

        @s.block.sync
        def _(sp):
            loads = [
                (net.x[:, :, :], a["x"].rearrange("(t p) f -> p t f", p=P)),
                (lw[:, :, :], a["L0_gnn_lin_weight"].rearrange("b o i -> o b i")),
                (mix[:, :], a["L0_gnn_coeffs_t"].partition_broadcast(P)),
                (wi[:, :], a["L3_gnn_W"]),
                (att[:, 0, :], a["L0_gnn_att_src"].rearrange("b q h c -> (q h c) b")),
                (att[:, 1, :], a["L0_gnn_att_dst"].rearrange("b q h c -> (q h c) b")),
                (att3[:, 0:1], a["L3_gnn_att_src"].rearrange("q h c -> (q h c)").unsqueeze(1)),
                (att3[:, 1:2], a["L3_gnn_att_dst"].rearrange("q h c -> (q h c)").unsqueeze(1)),
                (heads[:, :], a["heads"]),
                (bcols[:, :], a["L0_gnn_lin_bias"].rearrange("b o -> o b")),
                (brow3[:, :, :], a["L0_gnn_lin_bias"].unsqueeze(0)),
                (net.ident[:, :], a["ident"]),
                (net.iota_row[:, :], a["iota"].partition_broadcast(P)),
                (net.iota_col[:, :], a["iota"].unsqueeze(1)),
                (dst_i[:, :, :], a["dst_cols"].rearrange("g p t -> p g t")),
                (src_i[:, :, :], a["src_cols"].rearrange("g p t -> p g t")),
                (typ_i[:, :, :], a["type_cols"].rearrange("g p t -> p g t")),
                (net.base_i[:, :], a["dst_first"].unsqueeze(0)),
                (slow_i[:, :], a["window_starts"].partition_broadcast(P)),
                (net.ones_row[:, :], a["ones"].unsqueeze(0)),
            ]
            assert len(loads) == LOADS
            with nc.allow_non_contiguous_dma(reason="small weights, once"):
                for to, of in loads:
                    sp.dma_start(to, of).then_inc(s.loaded, 16)
                sp.wait_ge(s.index_done, 1)
                sp.dma_start(net.rel_index.rearrange("g p t -> p g t"), src_i[:, :, :]).then_inc(s.index_out, 16)
            sp.wait_ge(s.index_out, 16)

        @s.block.vector
        def _(dve):
            dve.wait_ge(s.loaded, 16 * LOADS)
            def mixed(out, parts):
                nc.vector.tensor_scalar(out, parts[0], mix[0:out.shape[0], 0:1], None, ALU.mult)
                for b in (1, 2):
                    dve.drain()
                    nc.vector.scalar_tensor_tensor(out, parts[b], mix[0:out.shape[0], b:b + 1], out, ALU.mult, ALU.add)
                dve.drain()
            mixed(wo[:, 0, :], [lw[:, b, :] for b in range(3)])
            for k in range(2):
                mixed(acol[:, 0, k:k + 1], [att[:, k, b:b + 1] for b in range(3)])
            mixed(bcol[:, :], [bcols[:, b:b + 1] for b in range(3)])
            for l in range(2):
                nc.vector.memset(net.gat_w[l][:, :], 0.0)
            dve.drain()
            mixed(row[:, 0:F], [brow3[:, b, :] for b in range(3)])
            nc.vector.tensor_copy(acol[:, 1, :], att3[:, :])
            dve.drain()
            for l in range(2):
                for k in range(2):
                    nc.vector.tensor_scalar(fold[:, l, k * H:k * H + H], heads[:, :], acol[:, l, k:k + 1], None, ALU.mult)
            nc.vector.tensor_copy(net.gat_w[1][:, 0:F], wi[:, :])
            dve.drain().then_inc(s.combined, 1)
            dve.wait_ge(s.turned, 1)
            nc.vector.tensor_copy(net.gat_w[0][:, 0:F], pt[:, 0, :])
            nc.vector.tensor_copy(wo[:, 1, :], pt[:, 1, :])
            dve.drain().then_inc(s.turned_copied, 1)
            dve.wait_ge(s.folded, 1)
            for l in range(2):
                nc.vector.tensor_copy(net.gat_w[l][:, AS:AS + 2 * H], pf[:, 16 * l:16 * l + 2 * H])
            nc.vector.tensor_copy(row[:, AS:AS + 2 * H], pf[0:1, 64:64 + 2 * H])
            nc.vector.memset(row[:, ONE:ONE + 1], 0.0)

            nc.vector.scalar_tensor_tensor(src_i[:, :, :].rearrange("p g t -> p (g t)"), src_i[:, :, :].rearrange("p g t -> p (g t)"),
                                           float(R), typ_i[:, :, :].rearrange("p g t -> p (g t)"), ALU.mult, ALU.add)
            dve.drain().then_inc(s.index_done, 1)

            nc.vector.tensor_copy(base_row[:, :], net.base_i[:, :])
            nc.vector.tensor_copy(net.slow_base[:, :], slow_i[:, :])
            dve.drain().then_inc(s.checked, 1)
            dve.wait_ge(s.check_copied, 1)
            nc.vector.tensor_copy(net.fast_base[:, :], pb[:, 0:sh.NG])
            nc.vector.tensor_copy(net.gat_row[:, :], pr[:, 0:TAB + 1])
            dve.drain()
            nc.vector.tensor_tensor(rel[:, :, :], dst_i[:, :, :], tiled(net.fast_base[:, :], sh.NG, T), ALU.subtract)
            dve.drain()
            flat = rel[:, :, :].rearrange("p g t -> p (g t)")
            nc.vector.tensor_reduce(worst[:, 0:1], flat, AX.X, ALU.max)
            nc.vector.tensor_reduce(worst[:, 1:2], flat, AX.X, ALU.min)
            dve.drain()
            nc.vector.tensor_scalar(worst[:, 0:1], worst[:, 0:1], 1.0 - P, None, ALU.add)
            nc.vector.tensor_scalar(worst[:, 1:2], worst[:, 1:2], -1.0, None, ALU.mult)
            dve.drain()
            nc.vector.tensor_tensor(worst[:, 0:1], worst[:, 0:1], worst[:, 1:2], ALU.max)
            dve.drain().then_inc(s.flag_max, 1)
            dve.wait_ge(s.flag_row, 1)
            nc.vector.tensor_scalar(net.fits[:, :], worst_all[0:1, :], 0.0, None, ALU.is_le)
            dve.drain()

        @s.block.gpsimd
        def _(pool):
            pool.wait_ge(s.flag_max, 1)
            nc.gpsimd.partition_all_reduce(worst_all[:, :], worst[:, 0:1], P, MAX_OVER_PARTITIONS).then_inc(s.flag_row, 1)

        @s.block.tensor
        def _(pe):
            pe.wait_ge(s.combined, 1)
            nc.tensor.transpose(pt[:, 0, :], wo[:, 0, :], net.ident[:, :])
            nc.tensor.transpose(pt[:, 1, :], wi[:, :], net.ident[:, :]).then_inc(s.turned, 1)
            pe.wait_ge(s.turned_copied, 1)
            nc.tensor.matmul(pf[:, 0:2 * H], wo[:, 0, :], fold[:, 0, :], start=True, stop=True)
            nc.tensor.matmul(pf[:, 16:16 + 2 * H], wo[:, 1, :], fold[:, 1, :], start=True, stop=True)
            nc.tensor.matmul(pf[0:1, 64:64 + 2 * H], bcol[:, :], fold[:, 0, :], start=True, stop=True).then_inc(s.folded, 1)
            pe.wait_ge(s.checked, 1)
            nc.tensor.matmul(pr[:, 0:TAB + 1], net.ones_row[:, :], row[:, :], start=True, stop=True)
            nc.tensor.matmul(pb[:, 0:sh.NG], net.ones_row[:, :], base_row[:, :], start=True, stop=True).then_inc(s.check_copied, 1)



def gat_tables(net, layer, keep_self):
    nc, sh = net.nc, net.sh
    names = ["x_staged", "x_turned", "xt_ready", "product", "evacuated", "stored",
             "bound", "bound_all", "adc_done", "adc_stored", "zero_done", "sp_passed"]
    with phase(net, names) as s:
        xb = s.sb("xb", [P, sh.NB, F])
        xt = s.sb("xt", [P, sh.NB, P])
        tab = s.sb("tab", [P, sh.NB, TAB])
        most = s.sb("most", [P, 2 * H])
        part = s.sb("part", [P, 2 * H])
        most_all = s.sb("most_all", [P, 2 * H])
        spread_all = s.sb("spread_all", [1, H + 1])
        work = s.sb("work", [P, sh.NT, H])
        zeros = s.sb("zeros", [P, 2 * H])
        px = s.ps("px", [P, 8, P])
        ph = s.ps("ph", [P, 8, 2 * P])
        w = net.gat_w[layer]
        table = net.gat_table.rearrange("(t p) c -> p t c", p=P)

        @s.block.scalar
        def _(act):
            with act.Fori(0, sh.NBATCH) as i:
                wait(act, s.x_turned, i)
                nc.scalar.copy(xb[:, :, :], net.x[:, bass.ds(i * sh.NB, sh.NB), :]).then_inc(s.x_staged, 1)
                act.wait_ge(s.x_turned, i + 1)
                wait(act, s.product, i)
                nc.scalar.copy(xt[:, :, :], px[:, 0:sh.NB, :]).then_inc(s.xt_ready, 1)

        @s.block.tensor
        def _(pe):
            with pe.Fori(0, sh.NBATCH) as i:
                pe.wait_ge(s.x_staged, i + 1)
                wait(pe, s.xt_ready, i)
                for t in range(sh.NB):
                    last = nc.tensor.transpose(px[:, t, :], xb[:, t, :], net.ident[:, :])
                last.then_inc(s.x_turned, 1)
                pe.wait_ge(s.xt_ready, i + 1)
                wait(pe, s.evacuated, i)
                for t in range(sh.NB):
                    last = nc.tensor.matmul(ph[:, t, 0:TAB + 1], xt[:, t, :], w[:, :], start=True, stop=True)
                last.then_inc(s.product, 1)

        @s.block.vector
        def _(dve):
            nc.vector.memset(tab[:, :, ONE:ONE + 1], 1.0)
            nc.vector.memset(tab[:, :, SUMS:TAB], 0.0)
            nc.vector.memset(most[:, 0:H], -BIG)
            nc.vector.memset(most[:, H:2 * H], BIG)
            dve.drain()
            with dve.Fori(0, sh.NBATCH) as i:
                dve.wait_ge(s.product, i + 1)
                wait(dve, s.stored, i * 16)
                tiles = bass.ds(i * sh.NB, sh.NB)
                def columns(lo, hi):
                    return ph[:, 0:sh.NB, lo:hi]
                def bias(lo, hi):
                    return over_tiles(net.gat_row[:, lo:hi], sh.NB, hi - lo)
                if layer == 0:
                    nc.vector.tensor_tensor(tab[:, :, 0:F], columns(0, F), bias(0, F), ALU.add)
                    nc.vector.tensor_tensor(tab[:, :, AS:SUMS], columns(AS, SUMS), bias(AS, SUMS), ALU.add)
                    nc.vector.tensor_tensor(net.adc[:, tiles, 0:H], columns(SUMS, SUMS + H), bias(SUMS, SUMS + H), ALU.add)
                else:
                    nc.vector.tensor_copy(tab[:, :, 0:F], columns(0, F))
                    nc.vector.tensor_copy(tab[:, :, AS:SUMS], columns(AS, SUMS))
                    nc.vector.tensor_copy(net.adc[:, tiles, 0:H], columns(SUMS, SUMS + H))
                dve.drain()
                nc.vector.tensor_reduce(part[:, 0:H], tab[:, :, AS:SUMS].rearrange("p t h -> p h t"), AX.X, ALU.max)
                nc.vector.tensor_reduce(part[:, H:2 * H], tab[:, :, AS:SUMS].rearrange("p t h -> p h t"), AX.X, ALU.min)
                if keep_self:
                    nc.vector.tensor_copy(net.h_self[:, tiles, :], columns(0, F))
                    nc.vector.tensor_copy(net.a_self[:, tiles, :], columns(AS, SUMS))
                dve.drain()
                nc.vector.tensor_tensor(most[:, 0:H], most[:, 0:H], part[:, 0:H], ALU.max)
                nc.vector.tensor_tensor(most[:, H:2 * H], most[:, H:2 * H], part[:, H:2 * H], ALU.min)
                dve.drain().then_inc(s.evacuated, 1)
            nc.vector.tensor_scalar(most[:, H:2 * H], most[:, H:2 * H], -1.0, None, ALU.mult)
            dve.drain().then_inc(s.bound, 1)
            nc.vector.memset(zeros[:, :], 0.0)
            dve.drain().then_inc(s.zero_done, 1)
            dve.wait_ge(s.bound_all, 1)
            nc.vector.tensor_tensor(work[:, :, :], net.adc[:, :, 0:H], over_tiles(most_all[:, 0:H], sh.NT, H), ALU.add)
            nc.vector.tensor_tensor(spread_all[:, 0:H], most_all[0:1, 0:H], most_all[0:1, H:2 * H], ALU.add)
            dve.drain()
            nc.vector.tensor_reduce(spread_all[:, H:H + 1], spread_all[:, 0:H], AX.X, ALU.max)
            dve.drain()
            nc.vector.tensor_scalar(net.narrow[:, :], spread_all[:, H:H + 1], SPREAD, None, ALU.is_le)
            nc.vector.scalar_tensor_tensor(net.adc[:, :, H:2 * H], work[:, :, :], SLOPE, work[:, :, :], ALU.mult, ALU.max)
            dve.drain().then_inc(s.adc_done, 1)

        @s.block.gpsimd
        def _(pool):
            nc.gpsimd.memset(net.acc[:, 0, :], 0.0)
            nc.gpsimd.memset(net.den[:, :], 0.0)
            pool.wait_ge(s.bound, 1)
            nc.gpsimd.partition_all_reduce(most_all[:, :], most[:, :], P, MAX_OVER_PARTITIONS).then_inc(s.bound_all, 1)

        @s.block.sync
        def _(sp):
            with sp.Fori(0, sh.NBATCH) as i:
                sp.wait_ge(s.evacuated, i + 1)
                sp.sem_inc(s.sp_passed, 1)
                sp.dma_start(table[:, bass.ds(i * sh.NB, sh.NB), :], tab[:, :, :]).then_inc(s.stored, 16)
            sp.wait_ge(s.zero_done, 1)
            sp.dma_start(net.adc_table[sh.NP:sh.NW, :], zeros[:, :]).then_inc(s.adc_stored, 16)
            sp.wait_ge(s.adc_done, 1)
            sp.dma_start(net.adc_table[0:sh.NP, :].rearrange("(t p) c -> p t c", p=P), net.adc[:, :, :]).then_inc(s.adc_stored, 16)
            sp.wait_ge(s.stored, sh.NBATCH * 16)
            sp.wait_ge(s.adc_stored, 32)


def segment_max(net, keep_self):
    nc, sh, a = net.nc, net.sh, net.ins
    names = ["started", "loaded", "gathered", "spread_over", "head_done", "c_done", "c_stored", "sp_passed",
             "pool_passed", "dve_passed"]
    with phase(net, names) as s:
        idx = s.sb("idx", [P, T], I32)
        drow = s.sb("drow", [P, GE], I32)
        rows = s.sb("rows", [P, T, TAB])
        away = s.sb("away", [P, GE])
        cand = s.sb("cand", [P, GE])
        best = s.sb("best", [P, 1])
        most = s.sb("most", [P, sh.NT, H])
        work = s.sb("work", [P, sh.NT, H])
        iota_base = s.sb("iota_base", [P, 1])
        p_as = s.ps("p_as", [P, GE])

        def where_wide(eng, body):
            narrow = eng.value_load(net.narrow[0:1, 0:1], min_val=0, max_val=1)
            with eng.If(narrow == 0):
                body()

        @s.block.sync
        def _(sp):
            def body():
                with sp.Fori(0, sh.NG) as g:
                    wait(sp, s.head_done, g * H)
                    sp.sem_inc(s.sp_passed, 1)
                    sp.dma_start(idx[:, :], a["src_cols"][bass.ds(g, 1), :, :].rearrange("g p t -> p (g t)")).then_inc(s.loaded, 16)
                    sp.dma_start(drow[:, :], a["dst_rows"][bass.ds(g, 1), :].rearrange("g e -> (g e)").partition_broadcast(P)).then_inc(s.loaded, 16)
                sp.wait_ge(s.c_done, 1)
                sp.dma_start(net.adc_table[0:sh.NP, :].rearrange("(t p) c -> p t c", p=P), net.adc[:, :, :]).then_inc(s.c_stored, 16)
                sp.wait_ge(s.c_stored, 16)
            where_wide(sp, body)

        @s.block.gpsimd
        def _(pool):
            def body():
                with pool.Fori(0, sh.NG) as g:
                    pool.wait_ge(s.loaded, (g + 1) * 32)
                    pool.sem_inc(s.pool_passed, 1)
                    for t in range(T):
                        pool.indirect_dma_start(
                            out=rows[:, t, :], out_offset=None, in_=net.gat_table[:, :],
                            in_offset=bass.IndirectOffsetOnAxis(ap=idx[:, t:t + 1], axis=0),
                        ).then_inc(s.gathered, 16)
            where_wide(pool, body)

        @s.block.tensor
        def _(pe):
            def body():
                with pe.Fori(0, sh.NG) as g:
                    pe.wait_ge(s.gathered, (g + 1) * 16 * T)
                    for h in range(H):
                        wait(pe, s.head_done, g * H + h)
                        for t in range(T):
                            last = nc.tensor.matmul(p_as[:, t * P:(t + 1) * P], rows[:, t, AS + h:AS + h + 1].broadcast_to([P, P]),
                                                    net.ident[:, :], start=True, stop=True)
                        last.then_inc(s.spread_over, 1)
            where_wide(pe, body)

        @s.block.vector
        def _(dve):
            def body():
                nc.vector.memset(most[:, :, :], -BIG)
                dve.drain()
                with dve.Fori(0, sh.NG) as g:
                    dve.wait_ge(s.loaded, (g + 1) * 32)
                    for h in range(H):
                        dve.wait_ge(s.spread_over, g * H + h + 1)
                        dve.sem_inc(s.dve_passed, 1)
                        with dve.Fori(0, sh.NT) as k:
                            nc.vector.tensor_tensor(iota_base[:, :], net.iota_col[:, :], net.slow_base[:, bass.ds(k, 1)], ALU.add)
                            dve.drain()
                            nc.vector.tensor_scalar(away[:, :], drow[:, :], iota_base[:, 0:1], -BIG, ALU.not_equal, ALU.mult)
                            dve.drain()
                            nc.vector.tensor_tensor(cand[:, :], away[:, :], p_as[:, :], ALU.add)
                            dve.drain()
                            nc.vector.tensor_reduce(best[:, :], cand[:, :], AX.X, ALU.max)
                            dve.drain()
                            nc.vector.tensor_tensor(most[:, bass.ds(k, 1), h], most[:, bass.ds(k, 1), h], best[:, :], ALU.max)
                            dve.drain()
                        dve.drain().then_inc(s.head_done, 1)
                if keep_self:
                    nc.vector.tensor_tensor(most[:, :, :], most[:, :, :], net.a_self[:, :, :], ALU.max)
                    dve.drain()
                nc.vector.tensor_scalar(most[:, :, :], most[:, :, :], -BIG / 4, None, ALU.max)
                dve.drain()
                nc.vector.tensor_tensor(work[:, :, :], most[:, :, :], net.adc[:, :, 0:H], ALU.add)
                dve.drain()
                nc.vector.scalar_tensor_tensor(net.adc[:, :, H:2 * H], work[:, :, :], SLOPE, work[:, :, :], ALU.mult, ALU.max)
                dve.drain().then_inc(s.c_done, 1)
            where_wide(dve, body)



def pick(eng, net, program):
    if net.only is not None:
        program(net.only)
        return
    fits = eng.value_load(net.fits[0:1, 0:1], min_val=0, max_val=1)
    with eng.If(fits == 1):
        program(True)
    with eng.Else():
        program(False)


def window(eng, net, st, fast):
    if not fast:
        return st.base
    return eng.value_load(net.base_i[0:1, bass.ds(st.group, 1)], min_val=0, max_val=net.sh.NP - 1)


def base_column(net, st, fast):
    table = net.fast_base if fast else net.slow_base
    return table[:, bass.ds(st.col, 1)]


def edge_pass(net, kind):
    nc, sh, a = net.nc, net.sh, net.ins
    gat, mlp, rel = (kind == k for k in ("gat", "mlp", "rel"))
    names = ["always", "weights_in", "onehot", "turned_onehot", "adc_gathered", "logits", "weights_ready",
             "messages", "summed", "sums_copied", "sums_turned", "added", "edge_product", "pre", "squared",
             "scaled", "hidden", "w1e_zero", "relative", "rsqrt_steps", "pool_passed", "sp_passed"]
    width = TAB if gat else HID if mlp else F
    rings = ["index_in", "operands_in", "gathered"]
    with phase(net, names, rings) as s:
        idx = s.sb("idx", [P, RING, T], I32)
        dsts = s.sb("dsts", [P, RING, T], I32)
        rows = s.sb("rows", [P, RING, T, width])
        reld = s.sb("reld", [P, RING, T])
        hot = s.sb("hot", [P, RING, T, P])
        if gat:
            drow = s.sb("drow", [P, RING, GE], I32)
            adw = s.sb("adw", [P, RING, 2 * H])
            hot_t = s.sb("hot_t", [P, 2, GE])
            iota_base = s.sb("iota_base", [P, 2])
            z = s.sb("z", [P, 2, T * H])
            z2 = s.sb("z2", [P, 2, T * H])
            sums = s.sb("sums", [P, 2, SUMS])
            p_adc = [s.ps(f"p_adc{k}", [P, T, 64]) for k in range(2)]
            p_sum = [s.ps(f"p_sum{k}", [P, 512]) for k in range(2)]
            p_turn = [s.ps(f"p_turn{k}", [P, 512]) for k in range(2)]
        if mlp:
            eat = s.sb("eat", [P, RING, T // STACK, P])
            w1e = s.sb("w1e", [P, STACK, HID])
            w1em = s.sb("w1em", [P, 1])
            gamma = s.sb("gamma", [P, HID])
            beta = s.sb("beta", [P, HID])
            junk = s.sb("junk", [P, T, HID])
            stats = s.sb("stats", [P, RING, 4, T])
            p_pre = [s.ps(f"p_pre{k}", [P, T // 2, HID]) for k in range(2)]
            p_sum = [s.ps(f"p_sum{k}", [P, 2, P]) for k in range(2)]
        if rel:
            p_sum = [s.ps(f"p_sum{k}", [P, 512]) for k in range(2)]

        table = net.gat_table if gat else net.mlp_table if mlp else net.rel_table
        indices = net.rel_index if rel else a["src_cols"]

        def depth(fast, k):
            return k if fast else 1

        @s.block.sync
        def _(sp):
            def load(st, fast):
                ring = depth(fast, RING)
                wait(sp, s.onehot, st.n - ring + 1)
                if gat:
                    wait(sp, s.turned_onehot, st.n - ring + 1)
                    wait(sp, s.adc_gathered, st.n - ring + 1)
                if mlp:
                    wait(sp, s.summed, st.n - ring + 1)
                wait(sp, s.gathered[st.slot], st.visit * 16 * T)
                sp.sem_inc(s.sp_passed, 1)
                sp.dma_start(idx[:, st.slot, :], indices[bass.ds(st.group, 1), :, :].rearrange("g p t -> p (g t)")).then_inc(s.index_in[st.slot], 16)
                sp.dma_start(dsts[:, st.slot, :], a["dst_cols"][bass.ds(st.group, 1), :, :].rearrange("g p t -> p (g t)")).then_inc(s.operands_in[st.slot], 16)
                if gat:
                    first = window(sp, net, st, fast)
                    sp.dma_start(drow[:, st.slot, :], a["dst_rows"][bass.ds(st.group, 1), :].rearrange("g e -> (g e)").partition_broadcast(P)).then_inc(s.operands_in[st.slot], 16)
                    sp.dma_start(adw[:, st.slot, :], net.adc_table[bass.ds(first, P), :]).then_inc(s.operands_in[st.slot], 16)
                if mlp:
                    sp.dma_start(eat[:, st.slot, :, :], a["edge_t"][bass.ds(st.group, 1), :, :, :].rearrange("g k h e -> k (g h) e")).then_inc(s.operands_in[st.slot], 16)

            if mlp:
                sp.wait_ge(s.w1e_zero, 1)
                for j in range(STACK):
                    sp.dma_start(w1e[j * ED:(j + 1) * ED, j, :], a["L1_gnn_W1"][F:F + ED, :]).then_inc(s.weights_in, 16)
                sp.dma_start(gamma[:, :], a["L1_gnn_g1"].partition_broadcast(P)).then_inc(s.weights_in, 16)
                sp.dma_start(beta[:, :], a["L1_gnn_be1"].partition_broadcast(P)).then_inc(s.weights_in, 16)
            pick(sp, net, lambda fast: drive(sp, sh, [(lambda st: load(st, fast), [0])], fast))

        operands = 48 if gat else 32 if mlp else 16

        @s.block.gpsimd
        def _(pool):
            def gather(st, fast):
                pool.wait_ge(s.index_in[st.slot], (st.visit + 1) * 16)
                wait(pool, s.summed, st.n - depth(fast, RING) + 1)
                pool.sem_inc(s.pool_passed, 1)
                for t in range(T):
                    pool.indirect_dma_start(
                        out=rows[:, st.slot, t, :], out_offset=None, in_=table[:, :],
                        in_offset=bass.IndirectOffsetOnAxis(ap=idx[:, st.slot, t:t + 1], axis=0),
                    ).then_inc(s.gathered[st.slot], 16)

            pick(pool, net, lambda fast: drive(pool, sh, [(lambda st: gather(st, fast), [0])], fast))

        @s.block.vector
        def _(dve):
            def one_hot_half(st, half):
                tt = slice(half * T // 2, (half + 1) * T // 2)
                return nc.vector.tensor_tensor(hot[:, st.slot, tt, :], tiled(reld[:, st.slot, tt], T // 2, P),
                                               over_tiles(net.iota_row[:, :], T // 2, P), ALU.is_equal)

            def relative(st, fast):
                dve.wait_ge(s.operands_in[st.slot], (st.visit + 1) * operands)
                wait(dve, s.summed, st.n - depth(fast, RING) + 1)
                return nc.vector.tensor_scalar(reld[:, st.slot, :], dsts[:, st.slot, :], base_column(net, st, fast), None, ALU.subtract)

            def one_hot(st, fast):
                k = st.slot % 2
                dve.wait_ge(s.operands_in[st.slot], (st.visit + 1) * operands)
                wait(dve, s.summed, st.n - depth(fast, RING) + 1)
                nc.vector.tensor_scalar(reld[:, st.slot, :], dsts[:, st.slot, :], base_column(net, st, fast), None, ALU.subtract)
                dve.drain()
                nc.vector.tensor_tensor(hot[:, st.slot, :, :], tiled(reld[:, st.slot, :], T, P), over_tiles(net.iota_row[:, :], T, P), ALU.is_equal).then_inc(s.onehot, 1)
                if gat:
                    wait(dve, s.adc_gathered, st.n - depth(fast, 2) + 1)
                    nc.vector.tensor_tensor(iota_base[:, k:k + 1], net.iota_col[:, :], base_column(net, st, fast), ALU.add)
                    dve.drain()
                    nc.vector.tensor_scalar(hot_t[:, k, :], drow[:, st.slot, :], iota_base[:, k:k + 1], None, ALU.is_equal).then_inc(s.turned_onehot, 1)

            def logits(st, fast):
                k = st.slot % 2
                dve.wait_ge(s.adc_gathered, st.n + 1)
                dve.wait_ge(s.gathered[st.slot], (st.visit + 1) * 16 * T)
                wait(dve, s.weights_ready, st.n - depth(fast, 2) + 1)
                zk = z[:, k, :].rearrange("p (t h) -> p t h", h=H)
                z2k = z2[:, k, :].rearrange("p (t h) -> p t h", h=H)
                nc.vector.tensor_tensor(zk, rows[:, st.slot, :, AS:AS + H], p_adc[k][:, :, 0:H], ALU.add)
                dve.drain()
                nc.vector.scalar_tensor_tensor(z2[:, k, :], z[:, k, :], SLOPE, z[:, k, :], ALU.mult, ALU.max)
                dve.drain()
                nc.vector.tensor_tensor(zk, z2k, p_adc[k][:, :, H:2 * H], ALU.subtract)
                dve.drain()
                nc.vector.tensor_scalar(z[:, k, :], z[:, k, :], 0.0, None, ALU.min).then_inc(s.logits, 1)

            def weigh(st, fast):
                dve.wait_ge(s.weights_ready, st.n + 1)
                hr = rows[:, st.slot, :, 0:F].rearrange("p t (h c) -> p t h c", c=C)
                wt = rows[:, st.slot, :, AS:AS + H].unsqueeze(3).broadcast_to([P, T, H, C])
                nc.vector.tensor_tensor(hr, hr, wt, ALU.mult).then_inc(s.messages, 1)

            def variance(st, j):
                var, y, work, half = (stats[:, st.slot, q, :] for q in range(4))
                if j == 0:
                    dve.wait_ge(s.squared, st.n + 1)
                    nc.vector.tensor_scalar(var, var, 1.0 / HID, EPS, ALU.mult, ALU.add).then_inc(s.rsqrt_steps, 1)
                else:
                    dve.wait_ge(s.rsqrt_steps, st.n * (RSQRT_STEPS + 1) + j)
                    rsqrt_step(nc, j - 1, y, work, var, half).then_inc(s.rsqrt_steps, 1)

            def pre_tile(st, t, fast):
                half, j = divmod(t, T // 2)
                if j == 0:
                    dve.wait_ge(s.edge_product, 2 * st.n + half + 1)
                nc.vector.tensor_tensor(rows[:, st.slot, t, :], rows[:, st.slot, t, :], p_pre[half][:, j, :], ALU.add).then_inc(s.pre, 1)

            def front(st, back, ago, fast):
                for j in range(RSQRT_STEPS + 1):
                    if back is not None and fast:
                        variance(back, j)
                    if st is not None and j == 0:
                        dve.wait_ge(s.gathered[st.slot], (st.visit + 1) * 16 * T)
                        relative(st, fast).then_inc(s.relative, 1)
                    if st is not None and j < T:
                        pre_tile(st, j, fast)
                    if st is not None and j == T:
                        dve.wait_ge(s.relative, st.n + 1)
                        one_hot_half(st, 0)
                    if st is not None and j == T + 1:
                        one_hot_half(st, 1).then_inc(s.onehot, 1)
                    if ago is not None and fast and j == T + 2:
                        add(ago, fast)

            def scale(st, fast):
                if not fast:
                    for j in range(RSQRT_STEPS + 1):
                        variance(st, j)
                dve.wait_ge(s.rsqrt_steps, (st.n + 1) * (RSQRT_STEPS + 1))
                for t in range(T):
                    nc.vector.scalar_tensor_tensor(rows[:, st.slot, t, :], rows[:, st.slot, t, :], stats[:, st.slot, 1, t:t + 1], gamma[:, :], ALU.mult, ALU.mult)
                dve.drain()
                nc.vector.tensor_tensor(rows[:, st.slot, :, :], rows[:, st.slot, :, :], over_tiles(beta[:, :], T, HID), ALU.add).then_inc(s.scaled, 1)

            def add(st, fast):
                k = st.slot % 2
                first = window(dve, net, st, fast)
                if gat:
                    dve.wait_ge(s.sums_turned, st.n + 1)
                    part, dpart = net.acc[:, 0, bass.ds(first, P)], net.den[:, bass.ds(first, P)]
                    nc.vector.tensor_tensor(part, part, p_turn[k][:, 0:P], ALU.add)
                    nc.vector.tensor_tensor(dpart, dpart, p_turn[k][0:1 + H, P:2 * P], ALU.add)
                elif mlp:
                    dve.wait_ge(s.summed, st.n + 1)
                    part = net.acc[:, :, bass.ds(first, P)]
                    nc.vector.tensor_tensor(part, part, p_sum[k][:, :, :], ALU.add)
                else:
                    dve.wait_ge(s.summed, st.n + 1)
                    part = net.acc[:, 0, bass.ds(first, P)]
                    nc.vector.tensor_tensor(part, part, p_sum[k][:, 0:P], ALU.add)
                dve.drain().then_inc(s.added, 1)

            if mlp:
                nc.vector.memset(w1e[:, :, :], 0.0)
                dve.drain().then_inc(s.w1e_zero, 1)
                dve.wait_ge(s.weights_in, 16 * (STACK + 2))
                for j in range(STACK):
                    block = w1e[j * ED:(j + 1) * ED, j, :]
                    mean = w1em[j * ED:(j + 1) * ED, :]
                    nc.vector.tensor_reduce(mean, block, AX.X, ALU.add)
                    dve.drain()
                    nc.vector.tensor_scalar(mean, mean, -1.0 / HID, None, ALU.mult)
                    dve.drain()
                    nc.vector.tensor_scalar(block, block, mean, None, ALU.add)
                    dve.drain()
            dve.drain().then_inc(s.always, 1)

            def program(fast):
                def of(stage):
                    return lambda *steps: stage(*steps, fast)
                if gat:
                    stages = [(of(logits), [1]), (of(one_hot), [0]), (of(weigh), [1]), (of(add), [2])]
                    if not fast:
                        stages = [(of(one_hot), [0]), (of(logits), [0]), (of(weigh), [0]), (of(add), [0])]
                elif mlp:
                    stages = [(of(front), [0, 1, 3]), (of(scale), [1])]
                    if not fast:
                        stages = [(of(front), [0, 0, 0]), (of(scale), [0]), (of(add), [0])]
                else:
                    stages = [(of(one_hot), [0]), (of(add), [1])]
                drive(dve, sh, stages, fast)
            pick(dve, net, program)

        @s.block.scalar
        def _(act):
            def weights(st, fast):
                k = st.slot % 2
                act.wait_ge(s.logits, st.n + 1)
                nc.scalar.activation(rows[:, st.slot, :, AS:AS + H], z[:, k, :].rearrange("p (t h) -> p t h", h=H), ACT.Exp).then_inc(s.weights_ready, 1)

            def copy_sums(st, fast):
                k = st.slot % 2
                act.wait_ge(s.summed, st.n + 1)
                wait(act, s.sums_turned, st.n - depth(fast, 2) + 1)
                nc.scalar.copy(sums[:, k, :], p_sum[k][:, 0:SUMS]).then_inc(s.sums_copied, 1)

            def square(st, fast):
                k = st.slot % 2
                wait(act, s.scaled, st.n - depth(fast, RING) + 1)
                for t in range(T):
                    if t % 4 == 0:
                        act.wait_ge(s.pre, T * st.n + t + 4)
                    nc.scalar.activation(junk[:, t, :], rows[:, st.slot, t, :], ACT.Square, accum_out=stats[:, st.slot, 0, t:t + 1])
                act.drain().then_inc(s.squared, 1)

            def gelu(st, fast):
                k = st.slot % 2
                act.wait_ge(s.scaled, st.n + 1)
                nc.scalar.activation(rows[:, st.slot, :, :], rows[:, st.slot, :, :], ACT.Gelu).then_inc(s.hidden, 1)

            def program(fast):
                def of(stage):
                    return lambda *steps: stage(*steps, fast)
                if gat:
                    stages = [(of(weights), [1]), (of(copy_sums), [1])]
                else:
                    stages = [(of(square), [0]), (of(gelu), [1 if fast else 0])]
                drive(act, sh, stages, fast)
            if not rel:
                pick(act, net, program)

        @s.block.tensor
        def _(pe):
            def spread_adc(st, fast):
                k = st.slot % 2
                pe.wait_ge(s.turned_onehot, st.n + 1)
                pe.wait_ge(s.operands_in[st.slot], (st.visit + 1) * operands)
                wait(pe, s.logits, st.n - depth(fast, 2) + 1)
                for t in range(T):
                    last = nc.tensor.matmul(p_adc[k][:, t, 0:2 * H], hot_t[:, k, t * P:(t + 1) * P], adw[:, st.slot, :], start=True, stop=True)
                last.then_inc(s.adc_gathered, 1)

            def edges(st, fast):
                pe.wait_ge(s.operands_in[st.slot], (st.visit + 1) * operands)
                for half in range(2):
                    wait(pe, s.pre, T * st.n - T // 2 * (1 - half) if fast else T * st.n)
                    for j in range(T // 2):
                        last = nc.tensor.matmul(p_pre[half][:, j, :], eat[:, st.slot, half, :], w1e[:, j, :], start=True, stop=True)
                    last.then_inc(s.edge_product, 1)

            def add_up(st, fast):
                k = st.slot % 2
                if gat:
                    pe.wait_ge(s.messages, st.n + 1)
                    wait(pe, s.sums_copied, st.n - depth(fast, 2) + 1)
                    for t in range(T):
                        last = nc.tensor.matmul(p_sum[k][:, 0:SUMS], hot[:, st.slot, t, :], rows[:, st.slot, t, 0:SUMS], start=(t == 0), stop=(t == T - 1))
                elif mlp:
                    pe.wait_ge(s.hidden, st.n + 1)
                    wait(pe, s.added, st.n - depth(fast, 2) + 1)
                    for b in range(2):
                        for t in range(T):
                            last = nc.tensor.matmul(p_sum[k][:, b, :], rows[:, st.slot, t, b * F:(b + 1) * F], hot[:, st.slot, t, :], start=(t == 0), stop=(t == T - 1))
                else:
                    pe.wait_ge(s.onehot, st.n + 1)
                    pe.wait_ge(s.gathered[st.slot], (st.visit + 1) * 16 * T)
                    wait(pe, s.added, st.n - depth(fast, 2) + 1)
                    for t in range(T):
                        last = nc.tensor.matmul(p_sum[k][:, 0:P], rows[:, st.slot, t, :], hot[:, st.slot, t, :], start=(t == 0), stop=(t == T - 1))
                last.then_inc(s.summed, 1)

            def turn(st, fast):
                k = st.slot % 2
                pe.wait_ge(s.sums_copied, st.n + 1)
                wait(pe, s.added, st.n - depth(fast, 2) + 1)
                nc.tensor.transpose(p_turn[k][:, 0:P], sums[:, k, 0:F], net.ident[:, :])
                nc.tensor.transpose(p_turn[k][0:1 + H, P:2 * P], sums[:, k, ONE:SUMS], net.ident[:, :]).then_inc(s.sums_turned, 1)

            def program(fast):
                def of(stage):
                    return lambda *steps: stage(*steps, fast)
                if gat:
                    stages = [(of(turn), [2]), (of(spread_adc), [0]), (of(add_up), [1])]
                    if not fast:
                        stages = [(of(spread_adc), [0]), (of(add_up), [0]), (of(turn), [0])]
                elif mlp:
                    stages = [(of(edges), [0]), (of(add_up), [2 if fast else 0])]
                else:
                    stages = [(of(add_up), [0])]
                drive(pe, sh, stages, fast)
            pe.wait_ge(s.always, 1)
            pick(pe, net, program)



def gat_finish(net, last):
    nc, sh, a = net.nc, net.sh, net.ins
    names = ["vec_in", "staged", "turned", "used", "e_logits", "e_ready", "done", "stored", "sp_passed"]
    with phase(net, names) as s:
        accb = s.sb("accb", [P, sh.NB, P])
        denb = s.sb("denb", [1 + H, sh.NB, P])
        o = s.sb("o", [P, sh.NB, F])
        sq = s.sb("sq", [P, sh.NB, F])
        stats = s.sb("stats", [P, 5, sh.NB])
        rd = s.sb("rd", [P, sh.NB, H])
        e = s.sb("e", [P, sh.NB, H])
        vec = s.sb("vec", [P, 3, F])
        pa = s.ps("pa", [P, 8, P])
        pd = s.ps("pd", [P, 8, 16])
        out = net.out.rearrange("(t p) f -> p t f", p=P)

        @s.block.sync
        def _(sp):
            if not last:
                return
            for k, name in enumerate(("bias", "gamma", "beta")):
                sp.dma_start(vec[:, k, :], a[f"L3_gnn_{name}"].partition_broadcast(P)).then_inc(s.vec_in, 16)
            with sp.Fori(0, sh.NBATCH) as i:
                sp.wait_ge(s.done, i + 1)
                sp.sem_inc(s.sp_passed, 1)
                sp.dma_start(out[:, bass.ds(i * sh.NB, sh.NB), :], net.x[:, bass.ds(i * sh.NB, sh.NB), :]).then_inc(s.stored, 16)
            sp.wait_ge(s.stored, sh.NBATCH * 16)

        @s.block.scalar
        def _(act):
            with act.Fori(0, sh.NBATCH) as i:
                wait(act, s.turned, i)
                nc.scalar.copy(accb[:, :, :], net.acc[:, 0, bass.ds(i * sh.BN, sh.BN)].rearrange("p (t n) -> p t n", n=P))
                nc.scalar.copy(denb[:, :, :], net.den[:, bass.ds(i * sh.BN, sh.BN)].rearrange("p (t n) -> p t n", n=P))
                act.drain().then_inc(s.staged, 1)
                if last:
                    act.wait_ge(s.e_logits, i + 1)
                    nc.scalar.activation(e[:, :, :], e[:, :, :], ACT.Exp).then_inc(s.e_ready, 1)

        @s.block.tensor
        def _(pe):
            with pe.Fori(0, sh.NBATCH) as i:
                pe.wait_ge(s.staged, i + 1)
                wait(pe, s.used, i)
                for t in range(sh.NB):
                    nc.tensor.transpose(pa[:, t, :], accb[:, t, :], net.ident[:, :])
                    end = nc.tensor.transpose(pd[:, t, 0:1 + H], denb[:, t, :], net.ident[0:1 + H, 0:1 + H])
                end.then_inc(s.turned, 1)

        @s.block.vector
        def _(dve):
            if last:
                dve.wait_ge(s.vec_in, 48)
            with dve.Fori(0, sh.NBATCH) as i:
                tiles = bass.ds(i * sh.NB, sh.NB)
                nb = sh.NB
                def by_head(ap):
                    return ap.rearrange("p t (h c) -> p t h c", c=C)
                def per_head(ap):
                    return ap.unsqueeze(3).broadcast_to([P, nb, H, C])
                if last:
                    nc.vector.tensor_tensor(rd[:, :, :], net.a_self[:, tiles, :], net.adc[:, tiles, 0:H], ALU.add)
                    dve.drain()
                    nc.vector.scalar_tensor_tensor(e[:, :, :], rd[:, :, :], SLOPE, rd[:, :, :], ALU.mult, ALU.max)
                    dve.drain()
                    nc.vector.tensor_tensor(e[:, :, :], e[:, :, :], net.adc[:, tiles, H:2 * H], ALU.subtract)
                    dve.drain().then_inc(s.e_logits, 1)
                    dve.wait_ge(s.e_ready, i + 1)
                    nc.vector.tensor_tensor(by_head(sq[:, :, :]), by_head(net.h_self[:, tiles, :]), per_head(e[:, :, :]), ALU.mult)
                dve.wait_ge(s.turned, i + 1)
                if last:
                    nc.vector.tensor_tensor(rd[:, :, :], pd[:, 0:nb, 1:1 + H], e[:, :, :], ALU.add)
                    dve.drain()
                    nc.vector.tensor_tensor(o[:, :, :], sq[:, :, :], pa[:, 0:nb, :], ALU.add)
                    nc.vector.tensor_scalar(rd[:, :, :], rd[:, :, :], SOFTMAX_EPS, None, ALU.add)
                else:
                    nc.vector.tensor_scalar(rd[:, :, :], pd[:, 0:nb, 1:1 + H], SOFTMAX_EPS, None, ALU.add)
                dve.drain()
                nc.vector.reciprocal(e[:, :, :], rd[:, :, :])
                dve.drain()
                if last:
                    nc.vector.tensor_tensor(by_head(o[:, :, :]), by_head(o[:, :, :]), per_head(e[:, :, :]), ALU.mult)
                else:
                    nc.vector.tensor_tensor(by_head(o[:, :, :]), by_head(pa[:, 0:nb, :]), per_head(e[:, :, :]), ALU.mult)
                dve.drain().then_inc(s.used, 1)
                if last:
                    nc.vector.tensor_tensor(o[:, :, :], o[:, :, :], over_tiles(vec[:, 0, :], nb, F), ALU.add)
                    dve.drain()
                    layer_norm(nc, o[:, :, :], o[:, :, :], sq[:, :, :], stats, nb)
                    dve.drain()
                    nc.vector.tensor_tensor(o[:, :, :], o[:, :, :], over_tiles(vec[:, 1, :], nb, F), ALU.mult)
                    dve.drain()
                    nc.vector.tensor_tensor(o[:, :, :], o[:, :, :], over_tiles(vec[:, 2, :], nb, F), ALU.add)
                    dve.drain()
                    nc.vector.scalar_tensor_tensor(o[:, :, :], o[:, :, :], 0.0, net.x[:, tiles, :], ALU.max, ALU.add)
                else:
                    nc.vector.tensor_tensor(o[:, :, :], o[:, :, :], net.x[:, tiles, :], ALU.add)
                dve.drain()
                layer_norm(nc, net.x[:, tiles, :], o[:, :, :], sq[:, :, :], stats, nb)
                dve.drain().then_inc(s.done, 1)


def mlp_tables(net):
    nc, sh, a = net.nc, net.sh, net.ins
    names = ["w_in", "w_done", "x_staged", "x_turned", "xt_ready", "product", "evacuated", "stored",
             "sp_passed"]
    with phase(net, names) as s:
        w = s.sb("w1x", [P, HID])
        b = s.sb("b1", [P, HID])
        m = s.sb("w_mean", [P, 2])
        xb = s.sb("xb", [P, sh.NB, F])
        xt = s.sb("xt", [P, sh.NB, P])
        tab = s.sb("tab", [P, sh.NB, HID])
        px = s.ps("px", [P, 8, P])
        ph = s.ps("ph", [P, 8, HID])
        table = net.mlp_table.rearrange("(t p) c -> p t c", p=P)

        @s.block.gpsimd
        def _(pool):
            nc.gpsimd.memset(net.acc[:, 0, :], 0.0)
            nc.gpsimd.memset(net.acc[:, 1, :], 0.0)

        @s.block.scalar
        def _(act):
            with act.Fori(0, sh.NBATCH) as i:
                wait(act, s.x_turned, i)
                nc.scalar.copy(xb[:, :, :], net.x[:, bass.ds(i * sh.NB, sh.NB), :]).then_inc(s.x_staged, 1)
                act.wait_ge(s.x_turned, i + 1)
                wait(act, s.product, i)
                nc.scalar.copy(xt[:, :, :], px[:, 0:sh.NB, :]).then_inc(s.xt_ready, 1)

        @s.block.tensor
        def _(pe):
            pe.wait_ge(s.w_done, 1)
            with pe.Fori(0, sh.NBATCH) as i:
                pe.wait_ge(s.x_staged, i + 1)
                wait(pe, s.xt_ready, i)
                for t in range(sh.NB):
                    last = nc.tensor.transpose(px[:, t, :], xb[:, t, :], net.ident[:, :])
                last.then_inc(s.x_turned, 1)
                pe.wait_ge(s.xt_ready, i + 1)
                wait(pe, s.evacuated, i)
                for t in range(sh.NB):
                    last = nc.tensor.matmul(ph[:, t, :], xt[:, t, :], w[:, :], start=True, stop=True)
                last.then_inc(s.product, 1)

        @s.block.vector
        def _(dve):
            dve.wait_ge(s.w_in, 32)
            nc.vector.tensor_reduce(m[:, 0:1], w[:, :], AX.X, ALU.add)
            nc.vector.tensor_reduce(m[:, 1:2], b[:, :], AX.X, ALU.add)
            dve.drain()
            nc.vector.tensor_scalar(m[:, :], m[:, :], -1.0 / HID, None, ALU.mult)
            dve.drain()
            nc.vector.tensor_scalar(w[:, :], w[:, :], m[:, 0:1], None, ALU.add)
            nc.vector.tensor_scalar(b[:, :], b[:, :], m[:, 1:2], None, ALU.add)
            dve.drain().then_inc(s.w_done, 1)
            with dve.Fori(0, sh.NBATCH) as i:
                dve.wait_ge(s.product, i + 1)
                wait(dve, s.stored, i * 16)
                nc.vector.tensor_tensor(tab[:, :, :], ph[:, 0:sh.NB, :], over_tiles(b[:, :], sh.NB, HID), ALU.add).then_inc(s.evacuated, 1)

        @s.block.sync
        def _(sp):
            sp.dma_start(w[:, :], a["L1_gnn_W1"][0:F, :]).then_inc(s.w_in, 16)
            sp.dma_start(b[:, :], a["L1_gnn_b1"].partition_broadcast(P)).then_inc(s.w_in, 16)
            with sp.Fori(0, sh.NBATCH) as i:
                sp.wait_ge(s.evacuated, i + 1)
                sp.sem_inc(s.sp_passed, 1)
                sp.dma_start(table[:, bass.ds(i * sh.NB, sh.NB), :], tab[:, :, :]).then_inc(s.stored, 16)
            sp.wait_ge(s.stored, sh.NBATCH * 16)


def mlp_finish(net):
    nc, sh, a = net.nc, net.sh, net.ins
    names = ["w_in", "b2_zero", "x_staged", "x_turned", "xt_ready", "agg", "agg_ready", "product", "read",
             "normed", "activated"]
    with phase(net, names) as s:
        w2 = s.sb("w2", [P, 2, F])
        b2 = s.sb("b2", [1 + H, F])
        wu = s.sb("wu", [P, 2, F])
        vec = s.sb("vec", [P, 3, F])
        xb = s.sb("xb", [P, sh.NB, F])
        xt = s.sb("xt", [P, sh.NB, P])
        at = s.sb("at", [P, 2, sh.BN // 2])
        o = s.sb("o", [P, sh.NB, F])
        sq = s.sb("sq", [P, sh.NB, F])
        stats = s.sb("stats", [P, 5, sh.NB])
        px = s.ps("px", [P, 8, P])
        pg = s.ps("pg", [P, 2, 512])
        pu = s.ps("pu", [P, 8, P])
        half = sh.BN // 2
        at_tiles = at[:, :, :].rearrange("p j n -> p (j n)").rearrange("p (t n) -> p t n", n=P)

        @s.block.sync
        def _(sp):
            sp.wait_ge(s.b2_zero, 1)
            for to, of in [(w2[:, :, :], a["L1_gnn_W2"].rearrange("(k p) o -> p k o", p=P)),
                           (b2[0:1, :], a["L1_gnn_b2"].unsqueeze(0)),
                           (wu[:, :, :], a["L1_gnn_Wu"].rearrange("(k p) o -> p k o", p=P)),
                           (vec[:, 2, :], a["L1_gnn_bu"].partition_broadcast(P)),
                           (vec[:, 0, :], a["L1_gnn_gu"].partition_broadcast(P)),
                           (vec[:, 1, :], a["L1_gnn_beu"].partition_broadcast(P))]:
                sp.dma_start(to, of).then_inc(s.w_in, 16)

        @s.block.scalar
        def _(act):
            with act.Fori(0, sh.NBATCH) as i:
                wait(act, s.x_turned, i)
                nc.scalar.copy(xb[:, :, :], net.x[:, bass.ds(i * sh.NB, sh.NB), :]).then_inc(s.x_staged, 1)
                act.wait_ge(s.x_turned, i + 1)
                wait(act, s.product, i)
                nc.scalar.copy(xt[:, :, :], px[:, 0:sh.NB, :]).then_inc(s.xt_ready, 1)
                act.wait_ge(s.agg, i + 1)
                nc.scalar.copy(at[:, :, :], pg[:, :, 0:half]).then_inc(s.agg_ready, 1)
                act.wait_ge(s.normed, i + 1)
                nc.scalar.activation(o[:, :, :], o[:, :, :], ACT.Gelu).then_inc(s.activated, 1)

        @s.block.tensor
        def _(pe):
            pe.wait_ge(s.w_in, 96)
            with pe.Fori(0, sh.NBATCH) as i:
                pe.wait_ge(s.x_staged, i + 1)
                wait(pe, s.xt_ready, i)
                for t in range(sh.NB):
                    last = nc.tensor.transpose(px[:, t, :], xb[:, t, :], net.ident[:, :])
                last.then_inc(s.x_turned, 1)
                wait(pe, s.agg_ready, i)
                for j in range(2):
                    nodes = bass.ds(i * sh.BN + j * half, half)
                    nc.tensor.matmul(pg[:, j, 0:half], w2[:, 0, :], net.acc[:, 0, nodes], start=True, stop=False)
                    nc.tensor.matmul(pg[:, j, 0:half], w2[:, 1, :], net.acc[:, 1, nodes], start=False, stop=False)
                    last = nc.tensor.matmul(pg[:, j, 0:half], b2[:, :], net.den[:, nodes], start=False, stop=True)
                last.then_inc(s.agg, 1)
                pe.wait_ge(s.xt_ready, i + 1)
                pe.wait_ge(s.agg_ready, i + 1)
                wait(pe, s.read, i)
                for t in range(sh.NB):
                    nc.tensor.matmul(pu[:, t, :], xt[:, t, :], wu[:, 0, :], start=True, stop=False)
                    last = nc.tensor.matmul(pu[:, t, :], at_tiles[:, t, :], wu[:, 1, :], start=False, stop=True)
                last.then_inc(s.product, 1)

        @s.block.vector
        def _(dve):
            nb = sh.NB
            nc.vector.memset(b2[:, :], 0.0)
            dve.drain().then_inc(s.b2_zero, 1)
            dve.wait_ge(s.w_in, 96)
            with dve.Fori(0, sh.NBATCH) as i:
                tiles = bass.ds(i * nb, nb)
                dve.wait_ge(s.product, i + 1)
                nc.vector.tensor_tensor(o[:, :, :], pu[:, 0:nb, :], over_tiles(vec[:, 2, :], nb, F), ALU.add)
                dve.drain().then_inc(s.read, 1)
                layer_norm(nc, o[:, :, :], o[:, :, :], sq[:, :, :], stats, nb)
                dve.drain()
                nc.vector.tensor_tensor(o[:, :, :], o[:, :, :], over_tiles(vec[:, 0, :], nb, F), ALU.mult)
                dve.drain()
                nc.vector.tensor_tensor(o[:, :, :], o[:, :, :], over_tiles(vec[:, 1, :], nb, F), ALU.add)
                dve.drain().then_inc(s.normed, 1)
                dve.wait_ge(s.activated, i + 1)
                nc.vector.tensor_tensor(o[:, :, :], o[:, :, :], net.x[:, tiles, :], ALU.add)
                dve.drain()
                nc.vector.tensor_tensor(o[:, :, :], o[:, :, :], net.x[:, tiles, :], ALU.add)
                dve.drain()
                layer_norm(nc, net.x[:, tiles, :], o[:, :, :], sq[:, :, :], stats, nb)
                dve.drain()


def rel_tables(net):
    nc, sh, a = net.nc, net.sh, net.ins
    names = ["w_in", "folded", "x_staged", "x_turned", "xt_ready", "product", "read", "scaled", "gate_ready",
             "stored0", "stored1", "sp_passed"]
    with phase(net, names) as s:
        w = s.sb("w", [P, R, F])
        b = s.sb("b", [P, R, F])
        gw = s.sb("gw", [P, R, F])
        wg = s.sb("wg", [P, R])
        bg = s.sb("bg", [1, R])
        gb = s.sb("gb", [1, R])
        work = s.sb("work", [P, R, F])
        xb = s.sb("xb", [P, sh.NB, F])
        xt = s.sb("xt", [P, sh.NB, P])
        gate = s.sb("gate", [P, 2, R])
        tab = s.sb("tab", [P, 2, R, F])
        px = s.ps("px", [P, 8, P])
        ph = [s.ps(f"ph{k}", [P, R, F]) for k in range(2)]
        pg = [s.ps(f"pg{k}", [P, 512]) for k in range(2)]
        stored = [s.stored0, s.stored1]
        table = net.rel_table.rearrange("(t p r) f -> t p (r f)", p=P, r=R)
        uses = [(sh.NB + 1) // 2, sh.NB // 2]

        @s.block.gpsimd
        def _(pool):
            nc.gpsimd.memset(net.acc[:, 0, :], 0.0)

        @s.block.scalar
        def _(act):
            with act.Fori(0, sh.NBATCH) as i:
                wait(act, s.x_turned, i)
                nc.scalar.copy(xb[:, :, :], net.x[:, bass.ds(i * sh.NB, sh.NB), :]).then_inc(s.x_staged, 1)
                act.wait_ge(s.x_turned, i + 1)
                nc.scalar.copy(xt[:, :, :], px[:, 0:sh.NB, :]).then_inc(s.xt_ready, 1)
                for t in range(sh.NB):
                    act.wait_ge(s.product, i * sh.NB + t + 1)
                    if t >= 2:
                        act.wait_ge(s.scaled, i * sh.NB + t - 1)
                    else:
                        wait(act, s.scaled, i * sh.NB)
                    nc.scalar.activation(gate[:, t % 2, :], pg[t % 2][:, 0:R], ACT.Sigmoid).then_inc(s.gate_ready, 1)

        @s.block.tensor
        def _(pe):
            pe.wait_ge(s.folded, 1)
            with pe.Fori(0, sh.NBATCH) as i:
                pe.wait_ge(s.x_staged, i + 1)
                for t in range(sh.NB):
                    last = nc.tensor.transpose(px[:, t, :], xb[:, t, :], net.ident[:, :])
                last.then_inc(s.x_turned, 1)
                pe.wait_ge(s.xt_ready, i + 1)
                for t in range(sh.NB):
                    k = t % 2
                    if t >= 2:
                        pe.wait_ge(s.read, i * sh.NB + t - 1)
                        pe.wait_ge(s.gate_ready, i * sh.NB + t - 1)
                    else:
                        wait(pe, s.read, i * sh.NB)
                        wait(pe, s.gate_ready, i * sh.NB)
                    for q in range(2):
                        four = slice(4 * q, 4 * q + 4)
                        out = ph[k][:, four, :].rearrange("p r f -> p (r f)")
                        nc.tensor.matmul(out, xt[:, t, :], w[:, four, :].rearrange("p r f -> p (r f)"), start=True, stop=True)
                    nc.tensor.matmul(pg[k][:, 0:R], xt[:, t, :], wg[:, :], start=True, stop=False)
                    nc.tensor.matmul(pg[k][:, 0:R], net.ones_row[:, :], bg[:, :], start=False, stop=True).then_inc(s.product, 1)

        @s.block.vector
        def _(dve):
            dve.wait_ge(s.w_in, 64)
            nc.vector.tensor_tensor(work[:, :, :], w[:, :, :], gw[:, :, :], ALU.mult)
            dve.drain()
            nc.vector.tensor_reduce(wg[:, :], work[:, :, :], AX.X, ALU.add)
            dve.drain()
            nc.vector.tensor_tensor(work[0:1, :, :], b[0:1, :, :], gw[0:1, :, :], ALU.mult)
            dve.drain()
            nc.vector.tensor_reduce(bg[:, :], work[0:1, :, :], AX.X, ALU.add)
            dve.drain()
            nc.vector.tensor_tensor(bg[:, :], bg[:, :], gb[:, :], ALU.add)
            dve.drain().then_inc(s.folded, 1)
            with dve.Fori(0, sh.NBATCH) as i:
                for t in range(sh.NB):
                    k = t % 2
                    dve.wait_ge(s.product, i * sh.NB + t + 1)
                    wait(dve, stored[k], (i * uses[k] + t // 2) * 16)
                    nc.vector.tensor_tensor(tab[:, k, :, :], ph[k][:, :, :], b[:, :, :], ALU.add).then_inc(s.read, 1)
                    dve.wait_ge(s.gate_ready, i * sh.NB + t + 1)
                    dve.wait_ge(s.read, i * sh.NB + t + 1)
                    nc.vector.tensor_tensor(tab[:, k, :, :], tab[:, k, :, :], tiled(gate[:, k, :], R, F), ALU.mult).then_inc(s.scaled, 1)

        @s.block.sync
        def _(sp):
            for to, of in [(w[:, :, :], a["L2_gnn_W"].rearrange("r i o -> i r o")),
                           (b[:, :, :], a["L2_gnn_bias_term"].rearrange("r o -> (r o)").partition_broadcast(P).rearrange("p (r o) -> p r o", r=R)),
                           (gw[:, :, :], a["L2_gnn_gate_weight"].rearrange("r o q -> (r o q)").partition_broadcast(P).rearrange("p (r o) -> p r o", r=R)),
                           (gb[:, :], a["L2_gnn_gate_bias"].rearrange("r q -> (r q)").unsqueeze(0))]:
                sp.dma_start(to, of).then_inc(s.w_in, 16)
            with sp.Fori(0, sh.NBATCH) as i:
                for t in range(sh.NB):
                    sp.wait_ge(s.scaled, i * sh.NB + t + 1)
                    sp.sem_inc(s.sp_passed, 1)
                    sp.dma_start(table[bass.ds(i * sh.NB + t, 1), :, :].rearrange("t p c -> p (t c)"),
                                 tab[:, t % 2, :, :].rearrange("p r f -> p (r f)")).then_inc(stored[t % 2], 16)
            for k in range(2):
                sp.wait_ge(stored[k], sh.NBATCH * uses[k] * 16)


def rel_finish(net):
    nc, sh, a = net.nc, net.sh, net.ins
    names = ["w_in", "x_staged", "x_turned", "xt_ready", "product", "read"]
    with phase(net, names) as s:
        lw = s.sb("lw", [P, F])
        xb = s.sb("xb", [P, sh.NB, F])
        ab = s.sb("ab", [P, sh.NB, P])
        xt = s.sb("xt", [P, sh.NB, P])
        o = s.sb("o", [P, sh.NB, F])
        sq = s.sb("sq", [P, sh.NB, F])
        stats = s.sb("stats", [P, 5, sh.NB])
        px = s.ps("px", [P, 8, P])
        pu = s.ps("pu", [P, 8, P])

        @s.block.sync
        def _(sp):
            sp.dma_start(lw[:, :], a["L2_gnn_loop_weight"]).then_inc(s.w_in, 16)

        @s.block.scalar
        def _(act):
            with act.Fori(0, sh.NBATCH) as i:
                wait(act, s.product, i)
                nc.scalar.copy(xb[:, :, :], net.x[:, bass.ds(i * sh.NB, sh.NB), :]).then_inc(s.x_staged, 1)
                nc.scalar.copy(ab[:, :, :], net.acc[:, 0, bass.ds(i * sh.BN, sh.BN)].rearrange("p (t n) -> p t n", n=P))
                act.wait_ge(s.x_turned, i + 1)
                nc.scalar.copy(xt[:, :, :], px[:, 0:sh.NB, :])
                act.drain().then_inc(s.xt_ready, 1)

        @s.block.tensor
        def _(pe):
            pe.wait_ge(s.w_in, 16)
            with pe.Fori(0, sh.NBATCH) as i:
                pe.wait_ge(s.x_staged, i + 1)
                for t in range(sh.NB):
                    last = nc.tensor.transpose(px[:, t, :], xb[:, t, :], net.ident[:, :])
                last.then_inc(s.x_turned, 1)
                pe.wait_ge(s.xt_ready, i + 1)
                wait(pe, s.read, i)
                for t in range(sh.NB):
                    nc.tensor.matmul(pu[:, t, :], ab[:, t, :], net.ident[:, :], start=True, stop=False)
                    last = nc.tensor.matmul(pu[:, t, :], xt[:, t, :], lw[:, :], start=False, stop=True)
                last.then_inc(s.product, 1)

        @s.block.vector
        def _(dve):
            nb = sh.NB
            with dve.Fori(0, sh.NBATCH) as i:
                tiles = bass.ds(i * nb, nb)
                dve.wait_ge(s.product, i + 1)
                nc.vector.scalar_tensor_tensor(o[:, :, :], pu[:, 0:nb, :], 0.0, net.x[:, tiles, :], ALU.max, ALU.add)
                dve.drain().then_inc(s.read, 1)
                layer_norm(nc, net.x[:, tiles, :], o[:, :, :], sq[:, :, :], stats, nb)
                dve.drain()


def build(nc, sh, ins, out, only=None):
    with ExitStack() as ctx:
        net = Net(nc, ctx, sh, ins, out)
        net.only = only
        prepare(net)
        gat_tables(net, 0, keep_self=False)
        segment_max(net, keep_self=False)
        edge_pass(net, "gat")
        gat_finish(net, last=False)
        mlp_tables(net)
        edge_pass(net, "mlp")
        mlp_finish(net)
        rel_tables(net)
        edge_pass(net, "rel")
        rel_finish(net)
        gat_tables(net, 1, keep_self=True)
        segment_max(net, keep_self=True)
        edge_pass(net, "gat")
        gat_finish(net, last=True)


WEIGHTS = ["L0_gnn_coeffs_t", "L0_gnn_lin_weight", "L0_gnn_lin_bias", "L0_gnn_att_src", "L0_gnn_att_dst",
           "L1_gnn_W1", "L1_gnn_b1", "L1_gnn_g1", "L1_gnn_be1", "L1_gnn_W2", "L1_gnn_b2", "L1_gnn_Wu",
           "L1_gnn_bu", "L1_gnn_gu", "L1_gnn_beu", "L2_gnn_W", "L2_gnn_bias_term", "L2_gnn_gate_weight",
           "L2_gnn_gate_bias", "L2_gnn_loop_weight", "L3_gnn_W", "L3_gnn_att_src", "L3_gnn_att_dst",
           "L3_gnn_bias", "L3_gnn_gamma", "L3_gnn_beta"]


def layout(sh, inputs):
    def padded(a, n, fill):
        out = np.full((n,) + a.shape[1:], fill, a.dtype)
        out[:a.shape[0]] = a
        return out

    arrays = {k: np.ascontiguousarray(inputs[k]) for k in WEIGHTS}
    ep = sh.NG * GE
    src, dst, typ = (padded(np.asarray(inputs[k]), ep, fill) for k, fill in
                     (("src", sh.N), ("dst", sh.N), ("edge_type_8", 0)))
    edge = padded(np.asarray(inputs["edge_attr_32"]), ep, 0)
    arrays["x"] = padded(np.asarray(inputs["x"]), sh.NP, 0)
    for name, v in (("src_cols", src), ("dst_cols", dst), ("type_cols", typ)):
        arrays[name] = np.ascontiguousarray(v.reshape(sh.NG, T, P).transpose(0, 2, 1))
    arrays["dst_rows"] = dst.reshape(sh.NG, GE)
    arrays["dst_first"] = np.ascontiguousarray(dst[::GE])
    edge = edge.reshape(sh.NG, T // STACK, STACK, P, ED).transpose(0, 2, 4, 1, 3)
    arrays["edge_t"] = np.ascontiguousarray(edge).reshape(sh.NG, STACK * ED, T // STACK, P)
    arrays["window_starts"] = np.arange(sh.NT, dtype=np.int32) * P
    arrays["ident"] = np.eye(P, dtype=np.float32)
    arrays["iota"] = np.arange(P, dtype=np.float32)
    arrays["ones"] = np.ones(P, dtype=np.float32)
    arrays["heads"] = np.kron(np.eye(H), np.ones((C, 1))).astype(np.float32)
    return arrays


def program(nc, inputs, only=None):
    sh = shapes_of(inputs["x"].shape[0], inputs["src"].shape[0])
    arrays, aps = {}, {}
    for name, v in layout(sh, inputs).items():
        arrays[f"in_{name}"] = v
        aps[name] = nc.dram_tensor(f"in_{name}", v.shape, mybir.dt.from_np(v.dtype), kind="ExternalInput").ap()
    out = nc.dram_tensor("out", (sh.NP, F), F32, kind="ExternalOutput").ap()
    build(nc, sh, aps, out, only)
    return arrays


def kernel(**inputs):
    import concourse.bacc as bacc
    from concourse.bass_utils import run_bass_kernel_spmd

    nc = bacc.Bacc("TRN2", target_bir_lowering=False, num_devices=1)
    arrays = program(nc, inputs)
    r = run_bass_kernel_spmd(nc, [arrays], core_ids=[0])
    return r.results[0]["out"][:inputs["x"].shape[0]]
```

```python
import concourse.bass as bass
from concourse import mybir
import numpy as np
from collections import namedtuple
from contextlib import ExitStack, contextmanager


F32 = mybir.dt.float32
I32 = mybir.dt.int32
ALU = mybir.AluOpType
ACT = mybir.ActivationFunctionType
AX = mybir.AxisListType
MAX_OVER_PARTITIONS = bass.bass_isa.ReduceOp.max

P = 128
F = 128
H = 4
C = F // H
HID = 2 * F
ED = 32
R = 8
T = 8
STACK = P // 32
GE = T * P
HOT_ON_ACT = 3
RING = 4
ONE, AS = F, F + 1
TAB = AS + 2 * H
SUMS = AS + H
EPS = 1e-5
SOFTMAX_EPS = 1e-16
SLOPE = 0.2
SPREAD = 20.0
BIG = 3.0e38

Shapes = namedtuple("Shapes", "N E NT NP NW NG NB NBATCH BN")
Step = namedtuple("Step", "n slot visit group col base")


def shapes_of(n, e):
    nb = 7
    nbatch = n // (P * nb) + 1
    nbatch += 1 - nbatch % 2
    nt = nbatch * nb
    ng = -(-e // (GE * RING)) * RING
    return Shapes(n, e, nt, nt * P, nt * P + P, ng, nb, nbatch, nb * P)


def wait(eng, sem, value):
    if isinstance(value, int) and value <= 0:
        return
    eng.wait_ge(sem, value)


def drive(eng, sh, stages, fast):
    if not fast:
        with eng.Fori(0, sh.NG) as g:
            with eng.Fori(0, sh.NT) as k:
                for stage, lags in stages:
                    stage(*[Step(g * sh.NT + k, 0, g * sh.NT + k, g, k, k * P)] * len(lags))
        return

    def at(n, k, visit):
        for stage, lags in stages:
            steps = []
            for lag in lags:
                inside = not isinstance(n, int) or 0 <= n - lag < sh.NG
                steps.append(Step(n - lag, (k - lag) % RING, visit + (k - lag) // RING, n - lag, n - lag, None) if inside else None)
            if any(st is not None for st in steps):
                stage(*steps)

    most = max(max(lags) for _, lags in stages)
    for n in range(RING):
        at(n, n, 0)
    if sh.NG > RING:
        with eng.Fori(1, sh.NG // RING) as i:
            for k in range(RING):
                at(i * RING + k, k, i)
    for n in range(sh.NG, sh.NG + most):
        at(n, n % RING, n // RING)


def uses_before(i, k):
    return (i - k) // 2


def uses_of(sh, k):
    return (sh.NBATCH + 1 - k) // 2


def sweep(eng, sh, stages):
    def at(n, parity):
        for fn, lag in stages:
            if not isinstance(n, int) or 0 <= n - lag < sh.NBATCH:
                fn(n - lag, (parity - lag) % 2)

    peeled = min(3, sh.NBATCH)
    for n in range(peeled):
        at(n, n % 2)
    if sh.NBATCH > peeled:
        with eng.Fori(1, (sh.NBATCH - 1) // 2) as j:
            for step in (1, 2):
                at(j * 2 + step, step % 2)
    if max(lag for _, lag in stages) == 1:
        at(sh.NBATCH, sh.NBATCH % 2)


class Net:

    def __init__(self, nc, ctx, sh, ins, out):
        self.nc, self.ctx, self.sh, self.ins, self.out = nc, ctx, sh, ins, out
        self.phases = 0

        def sb(name, shape, dt=F32):
            return ctx.enter_context(nc.sbuf_tensor(name, shape, dt))

        self.x = sb("x_nodes", [P, sh.NT, F])
        self.acc = sb("acc_t", [P, 2, sh.NW])
        self.h_self = self.acc[:, 1, 0:sh.NT * P].rearrange("p (t f) -> p t f", f=F)
        self.den = sb("den_t", [1 + H, sh.NW])
        self.adc = sb("adc", [P, sh.NT, 2 * H])
        self.att = sb("att", [P, sh.NT, 2 * H])
        self.degree = sb("degree", [P, sh.NT])
        self.ident = sb("ident", [P, P])
        self.iota_row = sb("iota_row", [P, P])
        self.iota_col = sb("iota_col", [P, 1])
        self.ones_row = sb("ones_row", [1, P])
        self.gat_w = [sb(f"gat_w{l}", [P, TAB]) for l in range(2)]
        self.gat_row = sb("gat_row", [P, 2, TAB])
        self.fast_base = sb("fast_base", [P, sh.NG])
        self.slow_base = sb("slow_base", [P, sh.NT])
        self.base_i = sb("base_i", [1, sh.NG], I32)
        self.fits = sb("fits", [1, 1], I32)
        self.narrow = sb("narrow", [1, 1], I32)

        def dram(name, shape, dt=F32):
            return nc.dram_tensor(name, shape, dt, kind="Internal").ap()

        self.gat_table = dram("gat_table", (sh.NP, TAB))
        self.adc_table = dram("adc_table", (sh.NW, 2 * H))
        self.mlp_table = dram("mlp_table", (sh.NP, HID))
        self.rel_table = dram("rel_table", (sh.NP * R, F))
        self.rel_index = dram("rel_index", (P, sh.NG, T), I32)


@contextmanager
def phase(net, names, rings=()):
    nc = net.nc
    net.phases += 1
    tag = f"_{net.phases}"
    sems = {n: nc.alloc_semaphore(n + tag) for n in names}
    for n in rings:
        sems[n] = [nc.alloc_semaphore(f"{n}{i}{tag}") for i in range(RING)]
    handles = []
    for s in sems.values():
        handles += s if isinstance(s, list) else [s]
    with ExitStack() as ctx:
        def sb(name, shape, dt=F32):
            return ctx.enter_context(nc.sbuf_tensor(name + tag, shape, dt))

        def ps(name, shape):
            return ctx.enter_context(nc.psum_tensor(name + tag, shape, F32))

        scope = namedtuple("Scope", ["sb", "ps", "block"] + list(sems))
        with nc.Block() as block:
            yield scope(sb, ps, block, **sems)
    nc.clear_and_free_semaphores(handles)
    nc.all_engine_barrier()


def tiled(ap, n, width):
    return ap.unsqueeze(2).broadcast_to([P, n, width])


def over_tiles(ap, n, width):
    return ap.unsqueeze(1).broadcast_to([P, n, width])


def one_tile(buf, t):
    return buf[:, bass.ds(t, 1), :].rearrange("p t f -> p (t f)")


def moments(nc, sh, six, buf, i):
    for t in range(sh.NB):
        nc.vector.bn_stats(one_tile(six, i * sh.NB + t), one_tile(buf, i * sh.NB + t))


def norm_factors(nc, s, n, scale, shift, six, work):
    dve = nc.vector
    mean2, apart, square, var = (work[:, k, :] for k in range(4))
    dve.tensor_tensor(mean2, six[:, :, 1], six[:, :, 4], ALU.add)
    dve.tensor_tensor(apart, six[:, :, 1], six[:, :, 4], ALU.subtract)
    dve.tensor_tensor(var, six[:, :, 2], six[:, :, 5], ALU.add)
    dve.drain()
    dve.tensor_tensor(square, apart, apart, ALU.mult)
    dve.drain()
    dve.scalar_tensor_tensor(var, square, F / 4.0, var, ALU.mult, ALU.add)
    dve.drain()
    dve.tensor_scalar(var, var, 1.0 / F, EPS, ALU.mult, ALU.add)
    dve.drain()
    dve.reciprocal(square, var)
    dve.drain().then_inc(s.variance, 1)
    dve.wait_ge(s.rooted, n)
    dve.tensor_tensor(square, scale, scale, ALU.mult)
    dve.drain()
    dve.scalar_tensor_tensor(square, square, -0.5, var, ALU.mult, ALU.mult)
    dve.drain()
    dve.scalar_tensor_tensor(scale, square, 1.5, scale, ALU.add, ALU.mult)
    dve.drain()
    dve.scalar_tensor_tensor(shift, mean2, -0.5, scale, ALU.mult, ALU.mult)
    dve.drain().then_inc(s.factors, 1)


def root(nc, s, n, scale, work):
    nc.scalar.wait_ge(s.variance, n)
    nc.scalar.activation(scale, work[:, 2, :], ACT.Sqrt).then_inc(s.rooted, 1)
    nc.scalar.wait_ge(s.factors, n)


def normalise_on_act(nc, sh, out, buf, scale, shift, i):
    for t in range(sh.NB):
        tile = i * sh.NB + t
        last = nc.scalar.activation(one_tile(out, tile), one_tile(buf, tile), ACT.Identity,
                                    scale=scale[:, bass.ds(tile, 1)], bias=shift[:, bass.ds(tile, 1)])
    return last


def normalise_on_dve(nc, sh, out, buf, scale, shift, i):
    for t in range(sh.NB):
        tile = i * sh.NB + t
        last = nc.vector.tensor_scalar(one_tile(out, tile), one_tile(buf, tile), scale[:, bass.ds(tile, 1)],
                                       shift[:, bass.ds(tile, 1)], ALU.mult, ALU.add)
    return last



def prepare(net):
    nc, sh, a = net.nc, net.sh, net.ins
    names = ["loaded", "x_in", "combined", "turned", "turned_copied", "folded",
             "checked", "check_copied", "index_done", "index_out",
             "flag_max", "flag_row"]
    with phase(net, names) as s:
        lw = s.sb("lin_w", [P, 3, F])
        mix = s.sb("mix", [P, 3])
        wo = s.sb("w_out_in", [P, 2, F])
        wi = s.sb("w_in_out", [P, F])
        att = s.sb("att_cols", [P, 2, 3])
        att3 = s.sb("att3_cols", [P, 2])
        acol = s.sb("acol", [P, 2, 2])
        heads = s.sb("heads", [P, H])
        fold = s.sb("fold", [P, 2, 2 * H])
        bcols = s.sb("bias_cols", [P, 3])
        bcol = s.sb("bias_col", [P, 1])
        brow3 = s.sb("bias_rows", [1, 3, F])
        row = s.sb("row", [1, 2, TAB])
        dst_i = s.sb("dst_i", [P, sh.NG, T], I32)
        src_i = s.sb("src_i", [P, sh.NG, T], I32)
        typ_i = s.sb("typ_i", [P, sh.NG, T], I32)
        rel = s.sb("rel", [P, sh.NG, T])
        base_row = s.sb("base_row", [1, sh.NG])
        worst = s.sb("worst", [P, 2])
        worst_all = s.sb("worst_all", [P, 1])
        slow_i = s.sb("slow_i", [P, sh.NT], I32)
        pt = s.ps("pt", [P, 2, P])
        pf = s.ps("pf", [P, 512])
        pr = s.ps("pr", [P, 512])
        pb = s.ps("pb", [P, 512])
        LOADS = 19

        @s.block.sync
        def _(sp):
            loads = [
                (lw[:, :, :], a["L0_gnn_lin_weight"].rearrange("b o i -> o b i")),
                (mix[:, :], a["L0_gnn_coeffs_t"].partition_broadcast(P)),
                (wi[:, :], a["L3_gnn_W"]),
                (att[:, 0, :], a["L0_gnn_att_src"].rearrange("b q h c -> (q h c) b")),
                (att[:, 1, :], a["L0_gnn_att_dst"].rearrange("b q h c -> (q h c) b")),
                (att3[:, 0:1], a["L3_gnn_att_src"].rearrange("q h c -> (q h c)").unsqueeze(1)),
                (att3[:, 1:2], a["L3_gnn_att_dst"].rearrange("q h c -> (q h c)").unsqueeze(1)),
                (heads[:, :], a["heads"]),
                (bcols[:, :], a["L0_gnn_lin_bias"].rearrange("b o -> o b")),
                (brow3[:, :, :], a["L0_gnn_lin_bias"].unsqueeze(0)),
                (net.ident[:, :], a["ident"]),
                (net.iota_row[:, :], a["iota"].partition_broadcast(P)),
                (net.iota_col[:, :], a["iota"].unsqueeze(1)),
                (dst_i[:, :, :], a["dst_all"]),
                (src_i[:, :, :], a["src_all"]),
                (typ_i[:, :, :], a["type_all"]),
                (net.base_i[:, :], a["dst_first"].unsqueeze(0)),
                (slow_i[:, :], a["window_starts"].partition_broadcast(P)),
                (net.ones_row[:, :], a["ones"].unsqueeze(0)),
            ]
            assert len(loads) == LOADS
            with nc.allow_non_contiguous_dma(reason="small weights, once"):
                for to, of in loads:
                    sp.dma_start(to, of).then_inc(s.loaded, 16)
                sp.dma_start(net.x[:, :, :], a["x"].rearrange("(t p) f -> p t f", p=P)).then_inc(s.x_in, 16)
                sp.wait_ge(s.index_done, 1)
                sp.dma_start(net.rel_index, src_i[:, :, :]).then_inc(s.index_out, 16)
            sp.wait_ge(s.index_out, 16)
            sp.wait_ge(s.x_in, 16)

        @s.block.vector
        def _(dve):
            dve.wait_ge(s.loaded, 16 * LOADS)
            def mixed(out, parts):
                nc.vector.tensor_scalar(out, parts[0], mix[0:out.shape[0], 0:1], None, ALU.mult)
                for b in (1, 2):
                    dve.drain()
                    nc.vector.scalar_tensor_tensor(out, parts[b], mix[0:out.shape[0], b:b + 1], out, ALU.mult, ALU.add)
                dve.drain()
            mixed(wo[:, 0, :], [lw[:, b, :] for b in range(3)])
            for k in range(2):
                mixed(acol[:, 0, k:k + 1], [att[:, k, b:b + 1] for b in range(3)])
            mixed(bcol[:, :], [bcols[:, b:b + 1] for b in range(3)])
            for l in range(2):
                nc.vector.memset(net.gat_w[l][:, :], 0.0)
            dve.drain()
            nc.vector.memset(row[:, :, :], 0.0)
            dve.drain()
            mixed(row[:, 0, 0:F], [brow3[:, b, :] for b in range(3)])
            nc.vector.tensor_copy(acol[:, 1, :], att3[:, :])
            dve.drain()
            for l in range(2):
                for k in range(2):
                    nc.vector.tensor_scalar(fold[:, l, k * H:k * H + H], heads[:, :], acol[:, l, k:k + 1], None, ALU.mult)
            nc.vector.tensor_copy(net.gat_w[1][:, 0:F], wi[:, :])
            dve.drain().then_inc(s.combined, 1)
            dve.wait_ge(s.turned, 1)
            nc.vector.tensor_copy(net.gat_w[0][:, 0:F], pt[:, 0, :])
            nc.vector.tensor_copy(wo[:, 1, :], pt[:, 1, :])
            dve.drain().then_inc(s.turned_copied, 1)
            dve.wait_ge(s.folded, 1)
            for l in range(2):
                nc.vector.tensor_copy(net.gat_w[l][:, AS:AS + 2 * H], pf[:, 16 * l:16 * l + 2 * H])
            nc.vector.tensor_copy(row[:, 0, AS:AS + 2 * H], pf[0:1, 64:64 + 2 * H])
            nc.vector.memset(row[:, :, ONE:ONE + 1], 1.0)

            nc.vector.scalar_tensor_tensor(src_i[:, :, :].rearrange("p g t -> p (g t)"), src_i[:, :, :].rearrange("p g t -> p (g t)"),
                                           float(R), typ_i[:, :, :].rearrange("p g t -> p (g t)"), ALU.mult, ALU.add)
            dve.drain().then_inc(s.index_done, 1)

            nc.vector.tensor_copy(base_row[:, :], net.base_i[:, :])
            nc.vector.tensor_copy(net.slow_base[:, :], slow_i[:, :])
            dve.drain().then_inc(s.checked, 1)
            dve.wait_ge(s.check_copied, 1)
            nc.vector.tensor_copy(net.fast_base[:, :], pb[:, 0:sh.NG])
            nc.vector.tensor_copy(net.gat_row[:, :, :], pr[:, 0:2 * TAB].rearrange("p (l c) -> p l c", l=2))
            dve.drain()
            nc.vector.tensor_tensor(rel[:, :, :], dst_i[:, :, :], tiled(net.fast_base[:, :], sh.NG, T), ALU.subtract)
            dve.drain()
            flat = rel[:, :, :].rearrange("p g t -> p (g t)")
            nc.vector.tensor_reduce(worst[:, 0:1], flat, AX.X, ALU.max)
            nc.vector.tensor_reduce(worst[:, 1:2], flat, AX.X, ALU.min)
            dve.drain()
            nc.vector.tensor_scalar(worst[:, 0:1], worst[:, 0:1], 1.0 - P, None, ALU.add)
            nc.vector.tensor_scalar(worst[:, 1:2], worst[:, 1:2], -1.0, None, ALU.mult)
            dve.drain()
            nc.vector.tensor_tensor(worst[:, 0:1], worst[:, 0:1], worst[:, 1:2], ALU.max)
            dve.drain().then_inc(s.flag_max, 1)
            dve.wait_ge(s.flag_row, 1)
            nc.vector.tensor_scalar(net.fits[:, :], worst_all[0:1, :], 0.0, None, ALU.is_le)
            dve.drain()

        @s.block.gpsimd
        def _(pool):
            pool.wait_ge(s.flag_max, 1)
            nc.gpsimd.partition_all_reduce(worst_all[:, :], worst[:, 0:1], P, MAX_OVER_PARTITIONS).then_inc(s.flag_row, 1)

        @s.block.tensor
        def _(pe):
            pe.wait_ge(s.combined, 1)
            nc.tensor.transpose(pt[:, 0, :], wo[:, 0, :], net.ident[:, :])
            nc.tensor.transpose(pt[:, 1, :], wi[:, :], net.ident[:, :]).then_inc(s.turned, 1)
            pe.wait_ge(s.turned_copied, 1)
            nc.tensor.matmul(pf[:, 0:2 * H], wo[:, 0, :], fold[:, 0, :], start=True, stop=True)
            nc.tensor.matmul(pf[:, 16:16 + 2 * H], wo[:, 1, :], fold[:, 1, :], start=True, stop=True)
            nc.tensor.matmul(pf[0:1, 64:64 + 2 * H], bcol[:, :], fold[:, 0, :], start=True, stop=True).then_inc(s.folded, 1)
            pe.wait_ge(s.checked, 1)
            nc.tensor.matmul(pr[:, 0:2 * TAB], net.ones_row[:, :], row[:, :, :].rearrange("p l c -> p (l c)"), start=True, stop=True)
            nc.tensor.matmul(pb[:, 0:sh.NG], net.ones_row[:, :], base_row[:, :], start=True, stop=True).then_inc(s.check_copied, 1)



def halves(sh):
    return [slice(0, 4), slice(4, sh.NB)]


def turn_nodes(net, s, xb, xt, px):
    nc, sh = net.nc, net.sh

    def stage(i, k):
        wait(nc.gpsimd, s.x_turned, i - 1)
        nc.gpsimd.sem_inc(s.pool_passed, 1)
        nc.gpsimd.tensor_copy(xb[:, k, :, :], net.x[:, bass.ds(i * sh.NB, sh.NB), :]).then_inc(s.x_staged, 1)

    def turn(i, k):
        nc.tensor.wait_ge(s.x_staged, i + 1)
        wait(nc.tensor, s.xt_ready, i - 1)
        for t in range(sh.NB):
            last = nc.tensor.transpose(px[k][:, t, :], xb[:, k, t, :], net.ident[:, :])
        last.then_inc(s.x_turned, 1)

    def copy(i, k):
        nc.scalar.wait_ge(s.x_turned, i + 1)
        wait(nc.scalar, s.product, i - 1)
        nc.scalar.copy(xt[:, k, :, :], px[k][:, 0:sh.NB, :]).then_inc(s.xt_ready, 1)

    return stage, turn, copy


def gat_tables(net, layer, keep_self):
    nc, sh = net.nc, net.sh
    names = ["pool_passed", "x_staged", "x_turned", "xt_ready", "product", "half_product", "evacuated",
             "tab_done", "kept", "stored0", "stored1", "bound", "bound_all", "adc_done", "adc_stored", "zero_done", "sp_passed"]
    with phase(net, names) as s:
        xb = s.sb("xb", [P, 2, sh.NB, F])
        xt = s.sb("xt", [P, 2, sh.NB, P])
        tab = s.sb("tab", [P, 2, sh.NB, TAB])
        most = s.sb("most", [P, 2 * H])
        most_all = s.sb("most_all", [P, 2 * H])
        spread_all = s.sb("spread_all", [1, H + 1])
        work = s.sb("work", [P, sh.NT, H])
        zeros = s.sb("zeros", [P, 2 * H])
        px = [s.ps(f"px{k}", [P, 8, P]) for k in range(2)]
        ph = s.ps("ph", [P, 8, 2 * P])
        w = net.gat_w[layer]
        table = net.gat_table.rearrange("(t p) c -> p t c", p=P)
        stored = [s.stored0, s.stored1]
        stage, turn, copy = turn_nodes(net, s, xb, xt, px)

        @s.block.scalar
        def _(act):
            def keep(i, k):
                act.wait_ge(s.tab_done, i + 1)
                nc.scalar.copy(net.h_self[:, bass.ds(i * sh.NB, sh.NB), :], tab[:, k, :, 0:F]).then_inc(s.kept, 1)

            sweep(act, sh, [(copy, 0)] + ([(keep, 1)] if keep_self else []))

        @s.block.tensor
        def _(pe):
            def multiply(i, k):
                pe.wait_ge(s.xt_ready, i + 1)
                for q, half in enumerate(halves(sh)):
                    wait(pe, s.evacuated, 2 * i - 1 + q)
                    for t in range(half.start, half.stop):
                        last = nc.tensor.matmul(ph[:, t, 0:TAB], xt[:, k, t, :], w[:, :], start=True, stop=True)
                    last.then_inc(s.half_product, 1)
                pe.drain().then_inc(s.product, 1)

            sweep(pe, sh, [(turn, 0), (multiply, 1)])

        @s.block.vector
        def _(dve):
            nc.vector.memset(zeros[:, :], 0.0)
            dve.drain().then_inc(s.zero_done, 1)

            def evacuate(i, k):
                wait(dve, stored[k], uses_before(i, k) * 16)
                if keep_self:
                    wait(dve, s.kept, i - 1)
                for q, half in enumerate(halves(sh)):
                    dve.wait_ge(s.half_product, 2 * i + q + 1)
                    nc.vector.tensor_tensor(tab[:, k, half, :], ph[:, half, 0:TAB], over_tiles(net.gat_row[:, layer, :], half.stop - half.start, TAB), ALU.add).then_inc(s.evacuated, 1)
                dve.drain().then_inc(s.tab_done, 1)
                nc.vector.tensor_copy(net.att[:, bass.ds(i * sh.NB, sh.NB), :], tab[:, k, :, AS:TAB])

            sweep(dve, sh, [(evacuate, 0)])
            dve.drain()
            nc.vector.tensor_reduce(most[:, 0:H], net.att[:, :, 0:H].rearrange("p t h -> p h t"), AX.X, ALU.max)
            nc.vector.tensor_reduce(most[:, H:2 * H], net.att[:, :, 0:H].rearrange("p t h -> p h t"), AX.X, ALU.min)
            dve.drain()
            nc.vector.tensor_scalar(most[:, H:2 * H], most[:, H:2 * H], -1.0, None, ALU.mult)
            dve.drain().then_inc(s.bound, 1)
            nc.vector.tensor_copy(net.adc[:, :, 0:H], net.att[:, :, H:2 * H])
            dve.wait_ge(s.bound_all, 1)
            nc.vector.tensor_tensor(work[:, :, :], net.att[:, :, H:2 * H], over_tiles(most_all[:, 0:H], sh.NT, H), ALU.add)
            nc.vector.tensor_tensor(spread_all[:, 0:H], most_all[0:1, 0:H], most_all[0:1, H:2 * H], ALU.add)
            dve.drain()
            nc.vector.tensor_reduce(spread_all[:, H:H + 1], spread_all[:, 0:H], AX.X, ALU.max)
            dve.drain()
            nc.vector.tensor_scalar(net.narrow[:, :], spread_all[:, H:H + 1], SPREAD, None, ALU.is_le)
            nc.vector.scalar_tensor_tensor(net.adc[:, :, H:2 * H], work[:, :, :], SLOPE, work[:, :, :], ALU.mult, ALU.max)
            dve.drain().then_inc(s.adc_done, 1)

        @s.block.gpsimd
        def _(pool):
            sweep(pool, sh, [(stage, 0)])
            nc.gpsimd.memset(net.acc[:, 0, :], 0.0)
            nc.gpsimd.memset(net.den[:, :], 0.0)
            pool.wait_ge(s.bound, 1)
            nc.gpsimd.partition_all_reduce(most_all[:, :], most[:, :], P, MAX_OVER_PARTITIONS).then_inc(s.bound_all, 1)

        @s.block.sync
        def _(sp):
            def store(i, k):
                sp.wait_ge(s.tab_done, i + 1)
                sp.sem_inc(s.sp_passed, 1)
                sp.dma_start(table[:, bass.ds(i * sh.NB, sh.NB), :], tab[:, k, :, :]).then_inc(stored[k], 16)

            sp.wait_ge(s.zero_done, 1)
            sp.dma_start(net.adc_table[sh.NP:sh.NW, :], zeros[:, :]).then_inc(s.adc_stored, 16)
            sweep(sp, sh, [(store, 0)])
            sp.wait_ge(s.adc_done, 1)
            sp.dma_start(net.adc_table[0:sh.NP, :].rearrange("(t p) c -> p t c", p=P), net.adc[:, :, :]).then_inc(s.adc_stored, 16)
            for k in range(2):
                wait(sp, stored[k], uses_of(sh, k) * 16)
            sp.wait_ge(s.adc_stored, 32)


def segment_max(net, keep_self):
    nc, sh, a = net.nc, net.sh, net.ins
    names = ["loaded", "gathered", "spread_over", "head_done", "c_done", "c_stored", "sp_passed",
             "pool_passed", "dve_passed"]
    with phase(net, names) as s:
        idx = s.sb("idx", [P, T], I32)
        drow = s.sb("drow", [P, GE], I32)
        rows = s.sb("rows", [P, T, TAB])
        away = s.sb("away", [P, GE])
        cand = s.sb("cand", [P, GE])
        best = s.sb("best", [P, 1])
        most = s.sb("most", [P, sh.NT, H])
        work = s.sb("work", [P, sh.NT, H])
        iota_base = s.sb("iota_base", [P, 1])
        p_as = s.ps("p_as", [P, GE])

        def where_wide(eng, body):
            narrow = eng.value_load(net.narrow[0:1, 0:1], min_val=0, max_val=1)
            with eng.If(narrow == 0):
                body()

        @s.block.sync
        def _(sp):
            def body():
                with sp.Fori(0, sh.NG) as g:
                    wait(sp, s.head_done, g * H)
                    sp.sem_inc(s.sp_passed, 1)
                    sp.dma_start(idx[:, :], a["src_cols"][bass.ds(g, 1), :, :].rearrange("g p t -> p (g t)")).then_inc(s.loaded, 16)
                    sp.dma_start(drow[:, :], a["dst_rows"][bass.ds(g, 1), :].rearrange("g e -> (g e)").partition_broadcast(P)).then_inc(s.loaded, 16)
                sp.wait_ge(s.c_done, 1)
                sp.dma_start(net.adc_table[0:sh.NP, :].rearrange("(t p) c -> p t c", p=P), net.adc[:, :, :]).then_inc(s.c_stored, 16)
                sp.wait_ge(s.c_stored, 16)
            where_wide(sp, body)

        @s.block.gpsimd
        def _(pool):
            def body():
                with pool.Fori(0, sh.NG) as g:
                    pool.wait_ge(s.loaded, (g + 1) * 32)
                    pool.sem_inc(s.pool_passed, 1)
                    for t in range(T):
                        pool.indirect_dma_start(
                            out=rows[:, t, :], out_offset=None, in_=net.gat_table[:, :],
                            in_offset=bass.IndirectOffsetOnAxis(ap=idx[:, t:t + 1], axis=0),
                        ).then_inc(s.gathered, 16)
            where_wide(pool, body)

        @s.block.tensor
        def _(pe):
            def body():
                with pe.Fori(0, sh.NG) as g:
                    pe.wait_ge(s.gathered, (g + 1) * 16 * T)
                    for h in range(H):
                        wait(pe, s.head_done, g * H + h)
                        for t in range(T):
                            last = nc.tensor.matmul(p_as[:, t * P:(t + 1) * P], rows[:, t, AS + h:AS + h + 1].broadcast_to([P, P]),
                                                    net.ident[:, :], start=True, stop=True)
                        last.then_inc(s.spread_over, 1)
            where_wide(pe, body)

        @s.block.vector
        def _(dve):
            def body():
                nc.vector.memset(most[:, :, :], -BIG)
                dve.drain()
                with dve.Fori(0, sh.NG) as g:
                    dve.wait_ge(s.loaded, (g + 1) * 32)
                    for h in range(H):
                        dve.wait_ge(s.spread_over, g * H + h + 1)
                        dve.sem_inc(s.dve_passed, 1)
                        with dve.Fori(0, sh.NT) as k:
                            nc.vector.tensor_tensor(iota_base[:, :], net.iota_col[:, :], net.slow_base[:, bass.ds(k, 1)], ALU.add)
                            dve.drain()
                            nc.vector.tensor_scalar(away[:, :], drow[:, :], iota_base[:, 0:1], -BIG, ALU.not_equal, ALU.mult)
                            dve.drain()
                            nc.vector.tensor_tensor(cand[:, :], away[:, :], p_as[:, :], ALU.add)
                            dve.drain()
                            nc.vector.tensor_reduce(best[:, :], cand[:, :], AX.X, ALU.max)
                            dve.drain()
                            nc.vector.tensor_tensor(most[:, bass.ds(k, 1), h], most[:, bass.ds(k, 1), h], best[:, :], ALU.max)
                            dve.drain()
                        dve.drain().then_inc(s.head_done, 1)
                if keep_self:
                    nc.vector.tensor_tensor(most[:, :, :], most[:, :, :], net.att[:, :, 0:H], ALU.max)
                    dve.drain()
                nc.vector.tensor_scalar(most[:, :, :], most[:, :, :], -BIG / 4, None, ALU.max)
                dve.drain()
                nc.vector.tensor_tensor(work[:, :, :], most[:, :, :], net.adc[:, :, 0:H], ALU.add)
                dve.drain()
                nc.vector.scalar_tensor_tensor(net.adc[:, :, H:2 * H], work[:, :, :], SLOPE, work[:, :, :], ALU.mult, ALU.max)
                dve.drain().then_inc(s.c_done, 1)
            where_wide(dve, body)



def pick(eng, net, program):
    if net.only is not None:
        program(net.only)
        return
    fits = eng.value_load(net.fits[0:1, 0:1], min_val=0, max_val=1)
    with eng.If(fits == 1):
        program(True)
    with eng.Else():
        program(False)


def window(eng, net, st, fast):
    if not fast:
        return st.base
    return eng.value_load(net.base_i[0:1, bass.ds(st.group, 1)], min_val=0, max_val=net.sh.NP - 1)


def base_column(net, st, fast):
    table = net.fast_base if fast else net.slow_base
    return table[:, bass.ds(st.col, 1)]


def edge_pass(net, kind):
    nc, sh, a = net.nc, net.sh, net.ins
    gat, mlp, rel = (kind == k for k in ("gat", "mlp", "rel"))
    names = ["always", "weights_in", "onehot", "turned_onehot", "adc_gathered", "logits", "weights_ready",
             "messages", "summed", "sums_copied", "sums_turned", "added", "edge_product", "pre",
             "scaled", "hidden", "w1e_zero", "deviation", "onehot_rest", "pool_passed", "sp_passed"]
    width = TAB if gat else HID if mlp else F
    rings = ["index_in", "operands_in", "gathered"]
    with phase(net, names, rings) as s:
        idx = s.sb("idx", [P, RING, T], I32)
        dsts = s.sb("dsts", [P, RING, T], I32)
        rows = s.sb("rows", [P, RING, T, width])
        reld = s.sb("reld", [P, RING, T])
        hot = s.sb("hot", [P, RING, T, P])
        if gat:
            drow = s.sb("drow", [P, RING, GE], I32)
            adw = s.sb("adw", [P, RING, 2 * H])
            hot_t = s.sb("hot_t", [P, 2, GE])
            iota_base = s.sb("iota_base", [P, 2])
            z = s.sb("z", [P, 2, T * H])
            z2 = s.sb("z2", [P, 2, T * H])
            sums = s.sb("sums", [P, 2, SUMS])
            p_adc = [s.ps(f"p_adc{k}", [P, T, 64]) for k in range(2)]
            p_sum = [s.ps(f"p_sum{k}", [P, 512]) for k in range(2)]
            p_turn = [s.ps(f"p_turn{k}", [P, 512]) for k in range(2)]
        if mlp:
            eat = s.sb("eat", [P, RING, T // STACK, P])
            w1e = s.sb("w1e", [P, STACK, HID])
            w1em = s.sb("w1em", [P, 1])
            gamma = s.sb("gamma", [P, HID])
            beta = s.sb("beta", [P, HID])
            junk = s.sb("junk", [P, T, HID])
            stats = s.sb("stats", [P, RING, 2, T])
            eps = s.sb("eps", [P, 1])
            minus_iota = s.sb("minus_iota", [P, P])
            p_pre = [s.ps(f"p_pre{k}", [P, T // 2, HID]) for k in range(2)]
            p_sum = [s.ps(f"p_sum{k}", [P, 2, P]) for k in range(2)]
        if rel:
            p_sum = [s.ps(f"p_sum{k}", [P, 512]) for k in range(2)]

        table = net.gat_table if gat else net.mlp_table if mlp else net.rel_table
        indices = net.rel_index if rel else a["src_cols"].rearrange("g p t -> p g t")

        by_dve = T - HOT_ON_ACT if mlp else T

        def depth(fast, k):
            return k if fast else 1

        @s.block.sync
        def _(sp):
            def load(st, fast):
                ring = depth(fast, RING)
                wait(sp, s.onehot, st.n - ring + 1)
                if gat:
                    wait(sp, s.turned_onehot, st.n - ring + 1)
                    wait(sp, s.adc_gathered, st.n - ring + 1)
                if mlp:
                    wait(sp, s.summed, st.n - ring + 1)
                wait(sp, s.gathered[st.slot], st.visit * 16 * T)
                sp.sem_inc(s.sp_passed, 1)
                sp.dma_start(idx[:, st.slot, :], indices[:, bass.ds(st.group, 1), :].rearrange("p g t -> p (g t)")).then_inc(s.index_in[st.slot], 16)
                sp.dma_start(dsts[:, st.slot, :], a["dst_cols"][bass.ds(st.group, 1), :, :].rearrange("g p t -> p (g t)")).then_inc(s.operands_in[st.slot], 16)
                if gat:
                    first = window(sp, net, st, fast)
                    sp.dma_start(drow[:, st.slot, :], a["dst_rows"][bass.ds(st.group, 1), :].rearrange("g e -> (g e)").partition_broadcast(P)).then_inc(s.operands_in[st.slot], 16)
                    sp.dma_start(adw[:, st.slot, :], net.adc_table[bass.ds(first, P), :]).then_inc(s.operands_in[st.slot], 16)
                if mlp:
                    sp.dma_start(eat[:, st.slot, :, :], a["edge_t"][bass.ds(st.group, 1), :, :, :].rearrange("g k h e -> k (g h) e")).then_inc(s.operands_in[st.slot], 16)

            if mlp:
                sp.wait_ge(s.w1e_zero, 1)
                for j in range(STACK):
                    sp.dma_start(w1e[j * ED:(j + 1) * ED, j, :], a["L1_gnn_W1"][F:F + ED, :]).then_inc(s.weights_in, 16)
                sp.dma_start(gamma[:, :], a["L1_gnn_g1"].partition_broadcast(P)).then_inc(s.weights_in, 16)
                sp.dma_start(beta[:, :], a["L1_gnn_be1"].partition_broadcast(P)).then_inc(s.weights_in, 16)
            pick(sp, net, lambda fast: drive(sp, sh, [(lambda st: load(st, fast), [0])], fast))

        operands = 48 if gat else 32 if mlp else 16

        @s.block.gpsimd
        def _(pool):
            def gather(st, fast):
                pool.wait_ge(s.index_in[st.slot], (st.visit + 1) * 16)
                wait(pool, s.summed, st.n - depth(fast, RING) + 1)
                pool.sem_inc(s.pool_passed, 1)
                for t in range(T):
                    pool.indirect_dma_start(
                        out=rows[:, st.slot, t, :], out_offset=None, in_=table[:, :],
                        in_offset=bass.IndirectOffsetOnAxis(ap=idx[:, st.slot, t:t + 1], axis=0),
                    ).then_inc(s.gathered[st.slot], 16)

            pick(pool, net, lambda fast: drive(pool, sh, [(lambda st: gather(st, fast), [0])], fast))

        @s.block.vector
        def _(dve):
            def one_hot(st, fast):
                k = st.slot % 2
                dve.wait_ge(s.operands_in[st.slot], (st.visit + 1) * operands)
                wait(dve, s.summed, st.n - depth(fast, RING) + 1)
                nc.vector.tensor_scalar(reld[:, st.slot, :], dsts[:, st.slot, :], base_column(net, st, fast), None, ALU.subtract)
                dve.drain()
                nc.vector.tensor_tensor(hot[:, st.slot, 0:by_dve, :], tiled(reld[:, st.slot, 0:by_dve], by_dve, P), over_tiles(net.iota_row[:, :], by_dve, P), ALU.is_equal).then_inc(s.onehot, 1)
                if gat:
                    wait(dve, s.adc_gathered, st.n - depth(fast, 2) + 1)
                    nc.vector.tensor_tensor(iota_base[:, k:k + 1], net.iota_col[:, :], base_column(net, st, fast), ALU.add)
                    dve.drain()
                    nc.vector.tensor_scalar(hot_t[:, k, :], drow[:, st.slot, :], iota_base[:, k:k + 1], None, ALU.is_equal).then_inc(s.turned_onehot, 1)

            def logits(st, fast):
                k = st.slot % 2
                dve.wait_ge(s.adc_gathered, st.n + 1)
                dve.wait_ge(s.gathered[st.slot], (st.visit + 1) * 16 * T)
                wait(dve, s.weights_ready, st.n - depth(fast, 2) + 1)
                zk = z[:, k, :].rearrange("p (t h) -> p t h", h=H)
                z2k = z2[:, k, :].rearrange("p (t h) -> p t h", h=H)
                nc.vector.tensor_tensor(zk, rows[:, st.slot, :, AS:AS + H], p_adc[k][:, :, 0:H], ALU.add)
                dve.drain()
                nc.vector.scalar_tensor_tensor(z2[:, k, :], z[:, k, :], SLOPE, z[:, k, :], ALU.mult, ALU.max)
                dve.drain()
                nc.vector.tensor_tensor(zk, z2k, p_adc[k][:, :, H:2 * H], ALU.subtract)
                dve.drain()
                nc.vector.tensor_scalar(z[:, k, :], z[:, k, :], 0.0, None, ALU.min).then_inc(s.logits, 1)

            def weigh(st, fast):
                dve.wait_ge(s.weights_ready, st.n + 1)
                hr = rows[:, st.slot, :, 0:F].rearrange("p t (h c) -> p t h c", c=C)
                wt = rows[:, st.slot, :, AS:AS + H].unsqueeze(3).broadcast_to([P, T, H, C])
                nc.vector.tensor_tensor(hr, hr, wt, ALU.mult).then_inc(s.messages, 1)

            def pre(st, fast):
                dve.wait_ge(s.gathered[st.slot], (st.visit + 1) * 16 * T)
                for half in range(2):
                    dve.wait_ge(s.edge_product, 2 * st.n + half + 1)
                    tt = slice(half * T // 2, (half + 1) * T // 2)
                    nc.vector.tensor_tensor(rows[:, st.slot, tt, :], rows[:, st.slot, tt, :], p_pre[half][:, :, :], ALU.add).then_inc(s.pre, 1)

            def scale(st, fast):
                dve.wait_ge(s.deviation, st.n + 1)
                nc.vector.reciprocal(stats[:, st.slot, 1, :], stats[:, st.slot, 0, :])
                dve.drain()
                for t in range(T):
                    nc.vector.scalar_tensor_tensor(rows[:, st.slot, t, :], rows[:, st.slot, t, :], stats[:, st.slot, 1, t:t + 1], gamma[:, :], ALU.mult, ALU.mult)
                dve.drain()
                nc.vector.tensor_tensor(rows[:, st.slot, :, :], rows[:, st.slot, :, :], over_tiles(beta[:, :], T, HID), ALU.add).then_inc(s.scaled, 1)

            def add(st, fast):
                k = st.slot % 2
                first = window(dve, net, st, fast)
                if gat:
                    dve.wait_ge(s.sums_turned, st.n + 1)
                    part, dpart = net.acc[:, 0, bass.ds(first, P)], net.den[:, bass.ds(first, P)]
                    nc.vector.tensor_tensor(part, part, p_turn[k][:, 0:P], ALU.add)
                    nc.vector.tensor_tensor(dpart, dpart, p_turn[k][0:1 + H, P:2 * P], ALU.add)
                elif mlp:
                    dve.wait_ge(s.summed, st.n + 1)
                    part = net.acc[:, :, bass.ds(first, P)]
                    nc.vector.tensor_tensor(part, part, p_sum[k][:, :, :], ALU.add)
                else:
                    dve.wait_ge(s.summed, st.n + 1)
                    part = net.acc[:, 0, bass.ds(first, P)]
                    nc.vector.tensor_tensor(part, part, p_sum[k][:, 0:P], ALU.add)
                dve.drain().then_inc(s.added, 1)

            if mlp:
                nc.vector.memset(eps[:, :], EPS)
                nc.vector.tensor_scalar(minus_iota[:, :], net.iota_row[:, :], -1.0, None, ALU.mult)
                nc.vector.memset(w1e[:, :, :], 0.0)
                dve.drain().then_inc(s.w1e_zero, 1)
                dve.wait_ge(s.weights_in, 16 * (STACK + 2))
                for j in range(STACK):
                    block = w1e[j * ED:(j + 1) * ED, j, :]
                    mean = w1em[j * ED:(j + 1) * ED, :]
                    nc.vector.tensor_reduce(mean, block, AX.X, ALU.add)
                    dve.drain()
                    nc.vector.tensor_scalar(mean, mean, -1.0 / HID, None, ALU.mult)
                    dve.drain()
                    nc.vector.tensor_scalar(block, block, mean, None, ALU.add)
                    dve.drain()
            dve.drain().then_inc(s.always, 1)

            def program(fast):
                def of(stage):
                    return lambda *steps: stage(*steps, fast)
                if gat:
                    stages = [(of(logits), [1]), (of(one_hot), [0]), (of(weigh), [1]), (of(add), [2])]
                    if not fast:
                        stages = [(of(one_hot), [0]), (of(logits), [0]), (of(weigh), [0]), (of(add), [0])]
                elif mlp:
                    stages = [(of(one_hot), [0]), (of(pre), [0]), (of(add), [3]), (of(scale), [1])]
                    if not fast:
                        stages = [(of(one_hot), [0]), (of(pre), [0]), (of(scale), [0]), (of(add), [0])]
                else:
                    stages = [(of(one_hot), [0]), (of(add), [1])]
                drive(dve, sh, stages, fast)
            pick(dve, net, program)

        @s.block.scalar
        def _(act):
            def weights(st, fast):
                k = st.slot % 2
                act.wait_ge(s.logits, st.n + 1)
                nc.scalar.activation(rows[:, st.slot, :, AS:AS + H], z[:, k, :].rearrange("p (t h) -> p t h", h=H), ACT.Exp).then_inc(s.weights_ready, 1)

            def copy_sums(st, fast):
                k = st.slot % 2
                act.wait_ge(s.summed, st.n + 1)
                wait(act, s.sums_turned, st.n - depth(fast, 2) + 1)
                nc.scalar.copy(sums[:, k, :], p_sum[k][:, 0:SUMS]).then_inc(s.sums_copied, 1)

            def square(st, fast):
                k = st.slot % 2
                wait(act, s.scaled, st.n - depth(fast, RING) + 1)
                for t in range(T):
                    if t % (T // 2) == 0:
                        act.wait_ge(s.pre, 2 * st.n + t // (T // 2) + 1)
                    nc.scalar.activation(junk[:, t, :], rows[:, st.slot, t, :], ACT.Square, accum_out=stats[:, st.slot, 0, t:t + 1])
                act.drain()
                nc.scalar.activation(stats[:, st.slot, 0, :], stats[:, st.slot, 0, :], ACT.Sqrt, scale=1.0 / HID, bias=eps[:, 0:1]).then_inc(s.deviation, 1)

            def one_hot(st, fast):
                act.wait_ge(s.onehot, st.n + 1)
                for t in range(by_dve, T):
                    nc.scalar.activation(hot[:, st.slot, t, :], minus_iota[:, :], ACT.Abs, bias=reld[:, st.slot, t:t + 1])
                act.drain()
                rest = hot[:, st.slot, by_dve:T, :]
                nc.scalar.activation(rest, rest, ACT.Relu, scale=-1.0, bias=1.0).then_inc(s.onehot_rest, 1)

            def gelu(st, fast):
                k = st.slot % 2
                act.wait_ge(s.scaled, st.n + 1)
                nc.scalar.activation(rows[:, st.slot, :, :], rows[:, st.slot, :, :], ACT.Gelu).then_inc(s.hidden, 1)

            def program(fast):
                def of(stage):
                    return lambda *steps: stage(*steps, fast)
                if gat:
                    stages = [(of(weights), [1]), (of(copy_sums), [1])]
                else:
                    stages = [(of(one_hot), [0]), (of(square), [0]), (of(gelu), [1 if fast else 0])]
                drive(act, sh, stages, fast)
            if not rel:
                pick(act, net, program)

        @s.block.tensor
        def _(pe):
            def spread_adc(st, fast):
                k = st.slot % 2
                pe.wait_ge(s.turned_onehot, st.n + 1)
                pe.wait_ge(s.operands_in[st.slot], (st.visit + 1) * operands)
                wait(pe, s.logits, st.n - depth(fast, 2) + 1)
                for t in range(T):
                    last = nc.tensor.matmul(p_adc[k][:, t, 0:2 * H], hot_t[:, k, t * P:(t + 1) * P], adw[:, st.slot, :], start=True, stop=True)
                last.then_inc(s.adc_gathered, 1)

            def edges(st, fast):
                pe.wait_ge(s.operands_in[st.slot], (st.visit + 1) * operands)
                for half in range(2):
                    wait(pe, s.pre, 2 * st.n - 1 + half if fast else 2 * st.n)
                    for j in range(T // 2):
                        last = nc.tensor.matmul(p_pre[half][:, j, :], eat[:, st.slot, half, :], w1e[:, j, :], start=True, stop=True)
                    last.then_inc(s.edge_product, 1)

            def add_up(st, fast):
                k = st.slot % 2
                if gat:
                    pe.wait_ge(s.messages, st.n + 1)
                    wait(pe, s.sums_copied, st.n - depth(fast, 2) + 1)
                    for t in range(T):
                        last = nc.tensor.matmul(p_sum[k][:, 0:SUMS], hot[:, st.slot, t, :], rows[:, st.slot, t, 0:SUMS], start=(t == 0), stop=(t == T - 1))
                elif mlp:
                    pe.wait_ge(s.hidden, st.n + 1)
                    pe.wait_ge(s.onehot_rest, st.n + 1)
                    wait(pe, s.added, st.n - depth(fast, 2) + 1)
                    for b in range(2):
                        for t in range(T):
                            last = nc.tensor.matmul(p_sum[k][:, b, :], rows[:, st.slot, t, b * F:(b + 1) * F], hot[:, st.slot, t, :], start=(t == 0), stop=(t == T - 1))
                else:
                    pe.wait_ge(s.onehot, st.n + 1)
                    pe.wait_ge(s.gathered[st.slot], (st.visit + 1) * 16 * T)
                    wait(pe, s.added, st.n - depth(fast, 2) + 1)
                    for t in range(T):
                        last = nc.tensor.matmul(p_sum[k][:, 0:P], rows[:, st.slot, t, :], hot[:, st.slot, t, :], start=(t == 0), stop=(t == T - 1))
                last.then_inc(s.summed, 1)

            def turn(st, fast):
                k = st.slot % 2
                pe.wait_ge(s.sums_copied, st.n + 1)
                wait(pe, s.added, st.n - depth(fast, 2) + 1)
                nc.tensor.transpose(p_turn[k][:, 0:P], sums[:, k, 0:F], net.ident[:, :])
                nc.tensor.transpose(p_turn[k][0:1 + H, P:2 * P], sums[:, k, ONE:SUMS], net.ident[:, :]).then_inc(s.sums_turned, 1)

            def program(fast):
                def of(stage):
                    return lambda *steps: stage(*steps, fast)
                if gat:
                    stages = [(of(turn), [2]), (of(spread_adc), [0]), (of(add_up), [1])]
                    if not fast:
                        stages = [(of(spread_adc), [0]), (of(add_up), [0]), (of(turn), [0])]
                elif mlp:
                    stages = [(of(edges), [0]), (of(add_up), [2 if fast else 0])]
                else:
                    stages = [(of(add_up), [0])]
                drive(pe, sh, stages, fast)
            pe.wait_ge(s.always, 1)
            pick(pe, net, program)



def gat_finish(net, last):
    nc, sh, a = net.nc, net.sh, net.ins
    names = ["vec_in", "staged", "turned", "used", "self_logits", "self_weights", "self_done", "variance", "rooted",
             "inner_normed", "factors", "act_normed", "dve_normed", "stored", "sp_passed"]
    with phase(net, names) as s:
        accb = s.sb("accb", [P, 2, sh.NB, P])
        denb = s.sb("denb", [1 + H, 2, sh.NB, P])
        six = s.sb("six", [P, sh.NT, 6])
        work = s.sb("work", [P, 4, sh.NT])
        scale = s.sb("scale", [P, sh.NT])
        shift = s.sb("shift", [P, sh.NT])
        rd = s.sb("rd", [P, sh.NB, H])
        share = s.sb("share", [P, sh.NB, H])
        if last:
            vec = s.sb("vec", [P, 3, F])
            e = s.sb("e", [P, sh.NT, H])
            loop_logit = s.sb("loop_logit", [P, sh.NT, H])
        o = s.sb("o", [P, sh.NT, F])
        pa = [s.ps(f"pa{k}", [P, 8, P]) for k in range(2)]
        pd = [s.ps(f"pd{k}", [P, 8, 64]) for k in range(2)]
        out = net.out.rearrange("(t p) f -> p t f", p=P)
        nb, nt = sh.NB, sh.NT
        on_act = max(1, sh.NBATCH // 2)

        @s.block.sync
        def _(sp):
            if not last:
                return
            for k, name in enumerate(("bias", "gamma", "beta")):
                sp.dma_start(vec[:, k, :], a[f"L3_gnn_{name}"].partition_broadcast(P)).then_inc(s.vec_in, 16)
            def store(i):
                sp.dma_start(out[:, bass.ds(i * nb, nb), :], net.x[:, bass.ds(i * nb, nb), :]).then_inc(s.stored, 16)
            with sp.Fori(0, on_act) as i:
                sp.wait_ge(s.act_normed, i + 1)
                sp.sem_inc(s.sp_passed, 1)
                store(i)
            if on_act < sh.NBATCH:
                sp.wait_ge(s.dve_normed, 1)
                sp.sem_inc(s.sp_passed, 1)
                with sp.Fori(on_act, sh.NBATCH) as i:
                    store(i)
            sp.wait_ge(s.stored, sh.NBATCH * 16)

        @s.block.gpsimd
        def _(pool):
            if not last:
                return
            pool.wait_ge(s.self_weights, 1)
            with pool.Fori(0, sh.NBATCH) as i:
                own = net.h_self[:, bass.ds(i * nb, nb), :].rearrange("p t (h c) -> p t h c", c=C)
                nc.gpsimd.tensor_tensor(own, own, e[:, bass.ds(i * nb, nb), :].unsqueeze(3).broadcast_to([P, nb, H, C]), ALU.mult).then_inc(s.self_done, 1)

        @s.block.scalar
        def _(act):
            if last:
                act.wait_ge(s.self_logits, 1)
                nc.scalar.activation(e[:, :, :], e[:, :, :], ACT.Exp).then_inc(s.self_weights, 1)

            def stage(i, k):
                wait(act, s.turned, i - 1)
                nc.scalar.copy(accb[:, k, :, :], net.acc[:, 0, bass.ds(i * sh.BN, sh.BN)].rearrange("p (t n) -> p t n", n=P))
                nc.scalar.copy(denb[:, k, :, :], net.den[:, bass.ds(i * sh.BN, sh.BN)].rearrange("p (t n) -> p t n", n=P))
                act.drain().then_inc(s.staged, 1)

            sweep(act, sh, [(stage, 0)])
            if last:
                root(nc, s, 1, scale[:, :], work)
                with act.Fori(0, sh.NBATCH) as i:
                    normalise_on_act(nc, sh, o, o, scale, shift, i)
                    act.drain().then_inc(s.inner_normed, 1)
            root(nc, s, 2 if last else 1, scale[:, :], work)
            with act.Fori(0, on_act) as i:
                normalise_on_act(nc, sh, net.x, net.x, scale, shift, i)
                act.drain().then_inc(s.act_normed, 1)

        @s.block.tensor
        def _(pe):
            def turn(i, k):
                pe.wait_ge(s.staged, i + 1)
                wait(pe, s.used, i - 1)
                for t in range(nb):
                    nc.tensor.transpose(pa[k][:, t, :], accb[:, k, t, :], net.ident[:, :])
                    end = nc.tensor.transpose(pd[k][:, t, 0:1 + H], denb[:, k, t, :], net.ident[0:1 + H, 0:1 + H])
                end.then_inc(s.turned, 1)

            sweep(pe, sh, [(turn, 0)])

        @s.block.vector
        def _(dve):
            def by_head(ap):
                return ap.rearrange("p t (h c) -> p t h c", c=C)

            def per_head(ap):
                return ap.unsqueeze(3).broadcast_to([P, nb, H, C])

            if last:
                nc.vector.tensor_tensor(loop_logit[:, :, :], net.att[:, :, 0:H], net.adc[:, :, 0:H], ALU.add)
                dve.drain()
                nc.vector.scalar_tensor_tensor(e[:, :, :], loop_logit[:, :, :], SLOPE, loop_logit[:, :, :], ALU.mult, ALU.max)
                dve.drain()
                nc.vector.tensor_tensor(e[:, :, :], e[:, :, :], net.adc[:, :, H:2 * H], ALU.subtract)
                dve.drain().then_inc(s.self_logits, 1)
                dve.wait_ge(s.self_weights, 1)
                dve.wait_ge(s.vec_in, 48)

            def divide(i, k):
                tiles = bass.ds(i * nb, nb)
                dve.wait_ge(s.turned, i + 1)
                if last:
                    dve.wait_ge(s.self_done, i + 1)
                    nc.vector.tensor_tensor(rd[:, :, :], pd[k][:, 0:nb, 1:1 + H], e[:, tiles, :], ALU.add)
                    nc.vector.tensor_tensor(o[:, tiles, :], net.h_self[:, tiles, :], pa[k][:, 0:nb, :], ALU.add)
                    dve.drain()
                    nc.vector.tensor_scalar(rd[:, :, :], rd[:, :, :], SOFTMAX_EPS, None, ALU.add)
                else:
                    nc.vector.tensor_scalar(rd[:, :, :], pd[k][:, 0:nb, 1:1 + H], SOFTMAX_EPS, None, ALU.add)
                    nc.vector.tensor_copy(net.degree[:, tiles], pd[k][:, 0:nb, 0])
                dve.drain()
                nc.vector.reciprocal(share[:, :, :], rd[:, :, :])
                dve.drain()
                sums = o[:, tiles, :] if last else pa[k][:, 0:nb, :]
                nc.vector.tensor_tensor(by_head(o[:, tiles, :]), by_head(sums), per_head(share[:, :, :]), ALU.mult)
                dve.drain().then_inc(s.used, 1)
                if last:
                    nc.vector.tensor_tensor(o[:, tiles, :], o[:, tiles, :], over_tiles(vec[:, 0, :], nb, F), ALU.add)
                    dve.drain()
                    moments(nc, sh, six, o, i)
                else:
                    nc.vector.tensor_tensor(net.x[:, tiles, :], o[:, tiles, :], net.x[:, tiles, :], ALU.add)
                    dve.drain()
                    moments(nc, sh, six, net.x, i)

            sweep(dve, sh, [(divide, 0)])
            dve.drain()
            if last:
                norm_factors(nc, s, 1, scale[:, :], shift[:, :], six, work)
                with dve.Fori(0, sh.NBATCH) as i:
                    tiles = bass.ds(i * nb, nb)
                    dve.wait_ge(s.inner_normed, i + 1)
                    nc.vector.tensor_tensor(o[:, tiles, :], o[:, tiles, :], over_tiles(vec[:, 1, :], nb, F), ALU.mult)
                    dve.drain()
                    nc.vector.tensor_tensor(o[:, tiles, :], o[:, tiles, :], over_tiles(vec[:, 2, :], nb, F), ALU.add)
                    dve.drain()
                    nc.vector.scalar_tensor_tensor(net.x[:, tiles, :], o[:, tiles, :], 0.0, net.x[:, tiles, :], ALU.max, ALU.add)
                    dve.drain()
                    moments(nc, sh, six, net.x, i)
                dve.drain()
            norm_factors(nc, s, 2 if last else 1, scale[:, :], shift[:, :], six, work)
            if on_act < sh.NBATCH:
                with dve.Fori(on_act, sh.NBATCH) as i:
                    normalise_on_dve(nc, sh, net.x, net.x, scale, shift, i)
                dve.drain().then_inc(s.dve_normed, 1)


def mlp_tables(net):
    nc, sh, a = net.nc, net.sh, net.ins
    names = ["w_in", "w_done", "pool_passed", "x_staged", "x_turned", "xt_ready", "product", "half_product", "evacuated",
             "stored0", "stored1", "sp_passed"]
    with phase(net, names) as s:
        w = s.sb("w1x", [P, HID])
        b = s.sb("b1", [P, HID])
        m = s.sb("w_mean", [P, 2])
        xb = s.sb("xb", [P, 2, sh.NB, F])
        xt = s.sb("xt", [P, 2, sh.NB, P])
        tab = s.sb("tab", [P, 2, sh.NB, HID])
        px = [s.ps(f"px{k}", [P, 8, P]) for k in range(2)]
        ph = s.ps("ph", [P, 8, HID])
        table = net.mlp_table.rearrange("(t p) c -> p t c", p=P)
        stored = [s.stored0, s.stored1]
        stage, turn, copy = turn_nodes(net, s, xb, xt, px)

        @s.block.gpsimd
        def _(pool):
            sweep(pool, sh, [(stage, 0)])
            nc.gpsimd.memset(net.acc[:, 0, :], 0.0)
            nc.gpsimd.memset(net.acc[:, 1, :], 0.0)

        @s.block.scalar
        def _(act):
            sweep(act, sh, [(copy, 0)])

        @s.block.tensor
        def _(pe):
            def multiply(i, k):
                pe.wait_ge(s.xt_ready, i + 1)
                for q, half in enumerate(halves(sh)):
                    wait(pe, s.evacuated, 2 * i - 1 + q)
                    for t in range(half.start, half.stop):
                        last = nc.tensor.matmul(ph[:, t, :], xt[:, k, t, :], w[:, :], start=True, stop=True)
                    last.then_inc(s.half_product, 1)
                pe.drain().then_inc(s.product, 1)

            pe.wait_ge(s.w_done, 1)
            sweep(pe, sh, [(turn, 0), (multiply, 1)])

        @s.block.vector
        def _(dve):
            def evacuate(i, k):
                wait(dve, stored[k], uses_before(i, k) * 16)
                for q, half in enumerate(halves(sh)):
                    dve.wait_ge(s.half_product, 2 * i + q + 1)
                    nc.vector.tensor_tensor(tab[:, k, half, :], ph[:, half, :], over_tiles(b[:, :], half.stop - half.start, HID), ALU.add).then_inc(s.evacuated, 1)

            dve.wait_ge(s.w_in, 32)
            nc.vector.tensor_reduce(m[:, 0:1], w[:, :], AX.X, ALU.add)
            nc.vector.tensor_reduce(m[:, 1:2], b[:, :], AX.X, ALU.add)
            dve.drain()
            nc.vector.tensor_scalar(m[:, :], m[:, :], -1.0 / HID, None, ALU.mult)
            dve.drain()
            nc.vector.tensor_scalar(w[:, :], w[:, :], m[:, 0:1], None, ALU.add)
            nc.vector.tensor_scalar(b[:, :], b[:, :], m[:, 1:2], None, ALU.add)
            dve.drain().then_inc(s.w_done, 1)
            sweep(dve, sh, [(evacuate, 0)])

        @s.block.sync
        def _(sp):
            def store(i, k):
                sp.wait_ge(s.evacuated, 2 * i + 2)
                sp.sem_inc(s.sp_passed, 1)
                sp.dma_start(table[:, bass.ds(i * sh.NB, sh.NB), :], tab[:, k, :, :]).then_inc(stored[k], 16)

            sp.dma_start(w[:, :], a["L1_gnn_W1"][0:F, :]).then_inc(s.w_in, 16)
            sp.dma_start(b[:, :], a["L1_gnn_b1"].partition_broadcast(P)).then_inc(s.w_in, 16)
            sweep(sp, sh, [(store, 0)])
            for k in range(2):
                wait(sp, stored[k], uses_of(sh, k) * 16)


def mlp_finish(net):
    nc, sh, a = net.nc, net.sh, net.ins
    names = ["w_in", "w2_turned", "w2_copied", "w2u", "w2u_ready", "pool_passed", "x_staged", "x_turned",
             "sums_staged", "xt_ready", "product", "read",
             "variance", "rooted", "normed", "scaled", "activated", "factors", "act_passed"]
    with phase(net, names) as s:
        w2 = s.sb("w2", [P, 2, F])
        w2t = s.sb("w2t", [P, 2, F])
        b2 = s.sb("b2", [P, 1])
        wu = s.sb("wu", [P, 2, F])
        w2u = s.sb("w2u", [P, 3, F])
        vec = s.sb("vec", [P, 3, F])
        xb = s.sb("xb", [P, 2, sh.NB, F])
        xt = s.sb("xt", [P, 2, sh.NB, P])
        sums = s.sb("sums", [P, 2, 2, sh.NB, P])
        o = s.sb("o", [P, sh.NT, F])
        six = s.sb("six", [P, sh.NT, 6])
        work = s.sb("work", [P, 4, sh.NT])
        scale = s.sb("scale", [P, sh.NT])
        shift = s.sb("shift", [P, sh.NT])
        px = [s.ps(f"px{k}", [P, 8, P]) for k in range(2)]
        pu = [s.ps(f"pu{k}", [P, 8, P]) for k in range(2)]
        nb = sh.NB
        on_act = max(1, sh.NBATCH // 2)
        stage, turn, copy = turn_nodes(net, s, xb, xt, px)

        @s.block.sync
        def _(sp):
            for to, of in [(w2[:, :, :], a["L1_gnn_W2"].rearrange("(k p) o -> p k o", p=P)),
                           (b2[:, :], a["L1_gnn_b2"].unsqueeze(1)),
                           (wu[:, :, :], a["L1_gnn_Wu"].rearrange("(k p) o -> p k o", p=P)),
                           (vec[:, 2, :], a["L1_gnn_bu"].partition_broadcast(P)),
                           (vec[:, 0, :], a["L1_gnn_gu"].partition_broadcast(P)),
                           (vec[:, 1, :], a["L1_gnn_beu"].partition_broadcast(P))]:
                sp.dma_start(to, of).then_inc(s.w_in, 16)

        @s.block.gpsimd
        def _(pool):
            sweep(pool, sh, [(stage, 0)])

        @s.block.scalar
        def _(act):
            def stage_sums(i, k):
                wait(act, s.product, i - 1)
                for b in range(2):
                    nc.scalar.copy(sums[:, k, b, :, :], net.acc[:, b, bass.ds(i * sh.BN, sh.BN)].rearrange("p (t n) -> p t n", n=P))
                act.drain().then_inc(s.sums_staged, 1)

            def normalise(i, k):
                normalise_on_act(nc, sh, o, o, scale, shift, i)
                act.drain().then_inc(s.normed, 1)

            def gelu(i, k):
                act.wait_ge(s.scaled, i + 1)
                act.sem_inc(s.act_passed, 1)
                nc.scalar.activation(o[:, bass.ds(i * nb, nb), :], o[:, bass.ds(i * nb, nb), :], ACT.Gelu).then_inc(s.activated, 1)

            sweep(act, sh, [(stage_sums, 0), (copy, 0)])
            root(nc, s, 1, scale[:, :], work)
            sweep(act, sh, [(normalise, 0), (gelu, 1)])
            root(nc, s, 2, scale[:, :], work)
            with act.Fori(0, on_act) as i:
                normalise_on_act(nc, sh, net.x, net.x, scale, shift, i)

        @s.block.tensor
        def _(pe):
            def multiply(i, k):
                pe.wait_ge(s.xt_ready, i + 1)
                pe.wait_ge(s.sums_staged, i + 1)
                wait(pe, s.read, i - 1)
                for t in range(nb):
                    nc.tensor.matmul(pu[k][:, t, :], xt[:, k, t, :], wu[:, 0, :], start=True, stop=False)
                    nc.tensor.matmul(pu[k][:, t, :], sums[:, k, 0, t, :], w2u[:, 0, :], start=False, stop=False)
                    last = nc.tensor.matmul(pu[k][:, t, :], sums[:, k, 1, t, :], w2u[:, 1, :], start=False, stop=True)
                last.then_inc(s.product, 1)

            pe.wait_ge(s.w_in, 96)
            for k in range(2):
                last = nc.tensor.transpose(pu[0][:, k, :], w2[:, k, :], net.ident[:, :])
            last.then_inc(s.w2_turned, 1)
            pe.wait_ge(s.w2_copied, 1)
            for k in range(2):
                nc.tensor.matmul(pu[1][:, k, :], w2t[:, k, :], wu[:, 1, :], start=True, stop=True)
            nc.tensor.matmul(pu[1][:, 2, :], b2[:, 0:1].broadcast_to([P, P]), wu[:, 1, :], start=True, stop=True).then_inc(s.w2u, 1)
            pe.wait_ge(s.w2u_ready, 1)
            sweep(pe, sh, [(turn, 0), (multiply, 1)])

        @s.block.vector
        def _(dve):
            def join(i, k):
                tiles = bass.ds(i * nb, nb)
                dve.wait_ge(s.product, i + 1)
                nc.vector.tensor_tensor(o[:, tiles, :], pu[k][:, 0:nb, :], over_tiles(vec[:, 2, :], nb, F), ALU.add)
                dve.drain().then_inc(s.read, 1)
                for t in range(nb):
                    tile = one_tile(o, i * nb + t)
                    nc.vector.scalar_tensor_tensor(tile, w2u[:, 2, :], net.degree[:, bass.ds(i * nb + t, 1)], tile, ALU.mult, ALU.add)
                dve.drain()
                moments(nc, sh, six, o, i)

            def affine(i, k):
                tiles = bass.ds(i * nb, nb)
                dve.wait_ge(s.normed, i + 1)
                nc.vector.tensor_tensor(o[:, tiles, :], o[:, tiles, :], over_tiles(vec[:, 0, :], nb, F), ALU.mult)
                dve.drain()
                nc.vector.tensor_tensor(o[:, tiles, :], o[:, tiles, :], over_tiles(vec[:, 1, :], nb, F), ALU.add)
                dve.drain().then_inc(s.scaled, 1)

            def residual(i, k):
                tiles = bass.ds(i * nb, nb)
                dve.wait_ge(s.activated, i + 1)
                nc.vector.scalar_tensor_tensor(net.x[:, tiles, :], net.x[:, tiles, :], 2.0, o[:, tiles, :], ALU.mult, ALU.add)
                dve.drain()
                moments(nc, sh, six, net.x, i)

            dve.wait_ge(s.w2_turned, 1)
            nc.vector.tensor_copy(w2t[:, :, :], pu[0][:, 0:2, :])
            dve.drain().then_inc(s.w2_copied, 1)
            dve.wait_ge(s.w2u, 1)
            nc.vector.tensor_copy(w2u[:, :, :], pu[1][:, 0:3, :])
            dve.drain().then_inc(s.w2u_ready, 1)
            sweep(dve, sh, [(join, 0)])
            dve.drain()
            norm_factors(nc, s, 1, scale[:, :], shift[:, :], six, work)
            sweep(dve, sh, [(affine, 0), (residual, 1)])
            dve.drain()
            norm_factors(nc, s, 2, scale[:, :], shift[:, :], six, work)
            if on_act < sh.NBATCH:
                with dve.Fori(on_act, sh.NBATCH) as i:
                    normalise_on_dve(nc, sh, net.x, net.x, scale, shift, i)


def rel_tables(net):
    nc, sh, a = net.nc, net.sh, net.ins
    names = ["w_in", "folded", "pool_passed", "x_staged", "x_turned", "xt_ready", "product", "read",
             "gate_product", "gate_logits", "gate_ready",
             "bias_product", "bias_copied",
             "dve_scaled", "act_scaled", "stored0", "stored1", "sp_passed"]
    with phase(net, names) as s:
        w = s.sb("w", [P, R, F])
        b = s.sb("b", [P, R, F])
        gw = s.sb("gw", [P, R, F])
        wg = s.sb("wg", [P, R])
        bg = s.sb("bg", [1, R])
        gb = s.sb("gb", [1, R])
        work = s.sb("work", [P, R, F])
        bg_all = s.sb("bg_all", [P, R])
        logit = s.sb("logit", [P, 2, sh.NB, R])
        xb = s.sb("xb", [P, 2, sh.NB, F])
        xt = s.sb("xt", [P, 2, sh.NB, P])
        gate = s.sb("gate", [P, 2, sh.NB, R])
        tab = s.sb("tab", [P, 2, sh.NB, R, F])
        px = s.ps("px", [P, 8, P])
        ph = [s.ps(f"ph{k}", [P, R, F]) for k in range(2)]
        pg = [s.ps(f"pg{k}", [P, sh.NB, 64]) for k in range(2)]
        stored = [s.stored0, s.stored1]
        table = net.rel_table.rearrange("(t p r) f -> t p (r f)", p=P, r=R)
        by_dve = 4

        def bank(k, t):
            return (k * sh.NB + t) % 2

        @s.block.gpsimd
        def _(pool):
            def stage(i, k):
                wait(pool, s.x_turned, i - 1)
                pool.sem_inc(s.pool_passed, 1)
                nc.gpsimd.tensor_copy(xb[:, k, :, :], net.x[:, bass.ds(i * sh.NB, sh.NB), :]).then_inc(s.x_staged, 1)

            sweep(pool, sh, [(stage, 0)])
            nc.gpsimd.memset(net.acc[:, 0, :], 0.0)

        @s.block.scalar
        def _(act):
            def copy(i, k):
                act.wait_ge(s.x_turned, i + 1)
                wait(act, s.product, (i - 1) * sh.NB)
                nc.scalar.copy(xt[:, k, :, :], px[:, 0:sh.NB, :]).then_inc(s.xt_ready, 1)

            def gates(i, k):
                act.wait_ge(s.gate_logits, i + 1)
                wait(act, stored[k], uses_before(i, k) * sh.NB * 16)
                nc.scalar.activation(gate[:, k, :, :], logit[:, k, :, :], ACT.Sigmoid).then_inc(s.gate_ready, 1)
                act.wait_ge(s.gate_ready, i + 1)
                for t in range(sh.NB):
                    act.wait_ge(s.read, i * sh.NB + t + 1)
                    for r in range(by_dve, R):
                        last = nc.scalar.activation(tab[:, k, t, r, :], tab[:, k, t, r, :], ACT.Copy, scale=gate[:, k, t, r:r + 1])
                    last.then_inc(s.act_scaled, 1)

            sweep(act, sh, [(copy, 0), (gates, 1)])

        @s.block.tensor
        def _(pe):
            def turn(i, k):
                pe.wait_ge(s.x_staged, i + 1)
                wait(pe, s.xt_ready, i)
                for t in range(sh.NB):
                    last = nc.tensor.transpose(px[:, t, :], xb[:, k, t, :], net.ident[:, :])
                last.then_inc(s.x_turned, 1)

            def multiply(i, k):
                pe.wait_ge(s.xt_ready, i + 1)
                wait(pe, s.gate_logits, i - 1)
                for t in range(sh.NB):
                    last = nc.tensor.matmul(pg[k][:, t, 0:R], xt[:, k, t, :], wg[:, :], start=True, stop=True)
                last.then_inc(s.gate_product, 1)
                for t in range(sh.NB):
                    j = bank(k, t)
                    wait(pe, s.read, i * sh.NB + t - 1)
                    for q in range(2):
                        four = slice(4 * q, 4 * q + 4)
                        out = ph[j][:, four, :].rearrange("p r f -> p (r f)")
                        last = nc.tensor.matmul(out, xt[:, k, t, :], w[:, four, :].rearrange("p r f -> p (r f)"), start=True, stop=True)
                    last.then_inc(s.product, 1)

            pe.wait_ge(s.folded, 1)
            nc.tensor.matmul(pg[0][:, 0, 0:R], net.ones_row[:, :], bg[:, :], start=True, stop=True).then_inc(s.bias_product, 1)
            pe.wait_ge(s.bias_copied, 1)
            sweep(pe, sh, [(turn, 0), (multiply, 1)])

        @s.block.vector
        def _(dve):
            def fill(i, k):
                dve.wait_ge(s.gate_product, i + 1)
                wait(dve, s.gate_ready, i - 1)
                nc.vector.tensor_tensor(logit[:, k, :, :], pg[k][:, :, 0:R], over_tiles(bg_all[:, :], sh.NB, R), ALU.add).then_inc(s.gate_logits, 1)
                wait(dve, stored[k], uses_before(i, k) * sh.NB * 16)
                for t in range(sh.NB):
                    dve.wait_ge(s.product, i * sh.NB + t + 1)
                    nc.vector.tensor_tensor(tab[:, k, t, :, :], ph[bank(k, t)][:, :, :], b[:, :, :], ALU.add).then_inc(s.read, 1)
                    dve.drain()
                    if t == 0:
                        dve.wait_ge(s.gate_ready, i + 1)
                    nc.vector.tensor_tensor(tab[:, k, t, 0:by_dve, :], tab[:, k, t, 0:by_dve, :], tiled(gate[:, k, t, 0:by_dve], by_dve, F), ALU.mult).then_inc(s.dve_scaled, 1)

            dve.wait_ge(s.w_in, 64)
            nc.vector.tensor_tensor(work[:, :, :], w[:, :, :], gw[:, :, :], ALU.mult)
            dve.drain()
            nc.vector.tensor_reduce(wg[:, :], work[:, :, :], AX.X, ALU.add)
            dve.drain()
            nc.vector.tensor_tensor(work[0:1, :, :], b[0:1, :, :], gw[0:1, :, :], ALU.mult)
            dve.drain()
            nc.vector.tensor_reduce(bg[:, :], work[0:1, :, :], AX.X, ALU.add)
            dve.drain()
            nc.vector.tensor_tensor(bg[:, :], bg[:, :], gb[:, :], ALU.add)
            dve.drain().then_inc(s.folded, 1)
            dve.wait_ge(s.bias_product, 1)
            nc.vector.tensor_copy(bg_all[:, :], pg[0][:, 0, 0:R])
            dve.drain().then_inc(s.bias_copied, 1)
            sweep(dve, sh, [(fill, 0)])

        @s.block.sync
        def _(sp):
            def store(i, k):
                for t in range(sh.NB):
                    sp.wait_ge(s.dve_scaled, i * sh.NB + t + 1)
                    sp.wait_ge(s.act_scaled, i * sh.NB + t + 1)
                    sp.sem_inc(s.sp_passed, 1)
                    sp.dma_start(table[bass.ds(i * sh.NB + t, 1), :, :].rearrange("t p c -> p (t c)"),
                                 tab[:, k, t, :, :].rearrange("p r f -> p (r f)")).then_inc(stored[k], 16)

            for to, of in [(w[:, :, :], a["L2_gnn_W"].rearrange("r i o -> i r o")),
                           (b[:, :, :], a["L2_gnn_bias_term"].rearrange("r o -> (r o)").partition_broadcast(P).rearrange("p (r o) -> p r o", r=R)),
                           (gw[:, :, :], a["L2_gnn_gate_weight"].rearrange("r o q -> (r o q)").partition_broadcast(P).rearrange("p (r o) -> p r o", r=R)),
                           (gb[:, :], a["L2_gnn_gate_bias"].rearrange("r q -> (r q)").unsqueeze(0))]:
                sp.dma_start(to, of).then_inc(s.w_in, 16)
            sweep(sp, sh, [(store, 0)])
            for k in range(2):
                wait(sp, stored[k], uses_of(sh, k) * sh.NB * 16)


def rel_finish(net):
    nc, sh, a = net.nc, net.sh, net.ins
    names = ["w_in", "pool_passed", "x_staged", "x_turned", "sums_staged", "xt_ready", "product", "read", "variance", "rooted", "factors"]
    with phase(net, names) as s:
        lw = s.sb("lw", [P, F])
        xb = s.sb("xb", [P, 2, sh.NB, F])
        sums = s.sb("sums", [P, 2, sh.NB, P])
        xt = s.sb("xt", [P, 2, sh.NB, P])
        six = s.sb("six", [P, sh.NT, 6])
        work = s.sb("work", [P, 4, sh.NT])
        scale = s.sb("scale", [P, sh.NT])
        shift = s.sb("shift", [P, sh.NT])
        px = [s.ps(f"px{k}", [P, 8, P]) for k in range(2)]
        pu = [s.ps(f"pu{k}", [P, 8, P]) for k in range(2)]
        nb = sh.NB
        on_act = max(1, sh.NBATCH // 2)
        stage, turn, copy = turn_nodes(net, s, xb, xt, px)

        @s.block.sync
        def _(sp):
            sp.dma_start(lw[:, :], a["L2_gnn_loop_weight"]).then_inc(s.w_in, 16)

        @s.block.gpsimd
        def _(pool):
            sweep(pool, sh, [(stage, 0)])

        @s.block.scalar
        def _(act):
            def stage_sums(i, k):
                wait(act, s.product, i - 1)
                nc.scalar.copy(sums[:, k, :, :], net.acc[:, 0, bass.ds(i * sh.BN, sh.BN)].rearrange("p (t n) -> p t n", n=P)).then_inc(s.sums_staged, 1)

            sweep(act, sh, [(stage_sums, 0), (copy, 0)])
            root(nc, s, 1, scale[:, :], work)
            with act.Fori(0, on_act) as i:
                normalise_on_act(nc, sh, net.x, net.x, scale, shift, i)

        @s.block.tensor
        def _(pe):
            def multiply(i, k):
                pe.wait_ge(s.xt_ready, i + 1)
                pe.wait_ge(s.sums_staged, i + 1)
                wait(pe, s.read, i - 1)
                for t in range(nb):
                    nc.tensor.matmul(pu[k][:, t, :], sums[:, k, t, :], net.ident[:, :], start=True, stop=False)
                    last = nc.tensor.matmul(pu[k][:, t, :], xt[:, k, t, :], lw[:, :], start=False, stop=True)
                last.then_inc(s.product, 1)

            pe.wait_ge(s.w_in, 16)
            sweep(pe, sh, [(turn, 0), (multiply, 1)])

        @s.block.vector
        def _(dve):
            def residual(i, k):
                tiles = bass.ds(i * nb, nb)
                dve.wait_ge(s.product, i + 1)
                nc.vector.scalar_tensor_tensor(net.x[:, tiles, :], pu[k][:, 0:nb, :], 0.0, net.x[:, tiles, :], ALU.max, ALU.add)
                dve.drain().then_inc(s.read, 1)
                moments(nc, sh, six, net.x, i)

            sweep(dve, sh, [(residual, 0)])
            dve.drain()
            norm_factors(nc, s, 1, scale[:, :], shift[:, :], six, work)
            if on_act < sh.NBATCH:
                with dve.Fori(on_act, sh.NBATCH) as i:
                    normalise_on_dve(nc, sh, net.x, net.x, scale, shift, i)


def build(nc, sh, ins, out, only=None):
    with ExitStack() as ctx:
        net = Net(nc, ctx, sh, ins, out)
        net.only = only
        prepare(net)
        gat_tables(net, 0, keep_self=False)
        segment_max(net, keep_self=False)
        edge_pass(net, "gat")
        gat_finish(net, last=False)
        mlp_tables(net)
        edge_pass(net, "mlp")
        mlp_finish(net)
        rel_tables(net)
        edge_pass(net, "rel")
        rel_finish(net)
        gat_tables(net, 1, keep_self=True)
        segment_max(net, keep_self=True)
        edge_pass(net, "gat")
        gat_finish(net, last=True)


WEIGHTS = ["L0_gnn_coeffs_t", "L0_gnn_lin_weight", "L0_gnn_lin_bias", "L0_gnn_att_src", "L0_gnn_att_dst",
           "L1_gnn_W1", "L1_gnn_b1", "L1_gnn_g1", "L1_gnn_be1", "L1_gnn_W2", "L1_gnn_b2", "L1_gnn_Wu",
           "L1_gnn_bu", "L1_gnn_gu", "L1_gnn_beu", "L2_gnn_W", "L2_gnn_bias_term", "L2_gnn_gate_weight",
           "L2_gnn_gate_bias", "L2_gnn_loop_weight", "L3_gnn_W", "L3_gnn_att_src", "L3_gnn_att_dst",
           "L3_gnn_bias", "L3_gnn_gamma", "L3_gnn_beta"]


def layout(sh, inputs):
    def padded(a, n, fill):
        out = np.full((n,) + a.shape[1:], fill, a.dtype)
        out[:a.shape[0]] = a
        return out

    arrays = {k: np.ascontiguousarray(inputs[k]) for k in WEIGHTS}
    ep = sh.NG * GE
    src, dst, typ = (padded(np.asarray(inputs[k]), ep, fill) for k, fill in
                     (("src", sh.N), ("dst", sh.N), ("edge_type_8", 0)))
    edge = padded(np.asarray(inputs["edge_attr_32"]), ep, 0)
    arrays["x"] = padded(np.asarray(inputs["x"]), sh.NP, 0)
    for name, v in (("src", src), ("dst", dst), ("type", typ)):
        arrays[name + "_all"] = np.ascontiguousarray(v.reshape(sh.NG, T, P).transpose(2, 0, 1))
    for name, v in (("src_cols", src), ("dst_cols", dst)):
        arrays[name] = np.ascontiguousarray(v.reshape(sh.NG, T, P).transpose(0, 2, 1))
    arrays["dst_rows"] = dst.reshape(sh.NG, GE)
    arrays["dst_first"] = np.ascontiguousarray(dst[::GE])
    edge = edge.reshape(sh.NG, T // STACK, STACK, P, ED).transpose(0, 2, 4, 1, 3)
    arrays["edge_t"] = np.ascontiguousarray(edge).reshape(sh.NG, STACK * ED, T // STACK, P)
    arrays["window_starts"] = np.arange(sh.NT, dtype=np.int32) * P
    arrays["ident"] = np.eye(P, dtype=np.float32)
    arrays["iota"] = np.arange(P, dtype=np.float32)
    arrays["ones"] = np.ones(P, dtype=np.float32)
    arrays["heads"] = np.kron(np.eye(H), np.ones((C, 1))).astype(np.float32)
    return arrays


def program(nc, inputs, only=None):
    sh = shapes_of(inputs["x"].shape[0], inputs["src"].shape[0])
    arrays, aps = {}, {}
    for name, v in layout(sh, inputs).items():
        arrays[f"in_{name}"] = v
        aps[name] = nc.dram_tensor(f"in_{name}", v.shape, mybir.dt.from_np(v.dtype), kind="ExternalInput").ap()
    out = nc.dram_tensor("out", (sh.NP, F), F32, kind="ExternalOutput").ap()
    build(nc, sh, aps, out, only)
    return arrays


def kernel(**inputs):
    import concourse.bacc as bacc
    from concourse.bass_utils import run_bass_kernel_spmd

    nc = bacc.Bacc("TRN2", target_bir_lowering=False, num_devices=1)
    arrays = program(nc, inputs)
    r = run_bass_kernel_spmd(nc, [arrays], core_ids=[0])
    return r.results[0]["out"][:inputs["x"].shape[0]]
```
